# Optimizing a Trainium2 kernel written in Bass

```python
import numpy as np
import jax
import jax.numpy as jnp

def _softmax(x, axis=-1):
    return jax.nn.softmax(x, axis=axis)

def _gelu(x):
    return jax.nn.gelu(x, approximate=True)

def _silu(x):
    return jax.nn.silu(x)

def _sigmoid(x):
    return jax.nn.sigmoid(x)

def _layernorm(x, axis=-1, eps=1e-05):
    m = jnp.mean(x, axis=axis, keepdims=True)
    v = jnp.var(x, axis=axis, keepdims=True)
    return (x - m) / jnp.sqrt(v + eps)

def _scatter_add(tgt, idx, src, axis=0):
    return tgt.at[idx].add(src)

def _segment_sum(src, seg, n):
    return jax.ops.segment_sum(src, seg, n)
kernel_name = 'mk_decoder_preln_d1_seqx_r8_7d9250'

def setup_inputs(seed: int=0):
    np.random.seed(seed)
    _w = jnp.asarray

    def _rec_inputs():
        import jax
        import jax.numpy as jnp
        _rk = jax.random.key(seed)
        x = -0.0002928 + 1 * jax.random.normal(jax.random.fold_in(_rk, 1), (8, 128, 128), jnp.float32)
        _lenS = 128 - jax.random.randint(jax.random.fold_in(_rk, 7), (8,), 0, max(1, 128 // 4) + 1, jnp.int32)
        _lenS2 = 128 - jax.random.randint(jax.random.fold_in(_rk, 8), (8,), 0, max(1, 128 // 4) + 1, jnp.int32)
        _ctx_1024P = jax.random.normal(jax.random.fold_in(_rk, 11), (8, 16, 128), jnp.float32)
        _ctx_1024c = jax.random.dirichlet(jax.random.fold_in(_rk, 511), 0.3 * jnp.ones((16,), jnp.float32), (8, 128))
        _ctx_1024t = jnp.einsum('bsk,bkd->bsd', _ctx_1024c, _ctx_1024P)
        _ctx_1024t = _ctx_1024t * jax.lax.rsqrt(jnp.mean(jnp.square(_ctx_1024t)) + 1e-12) * 0.953939
        ctx_1024 = -1.39393e-06 + 0.999914 * (_ctx_1024t + 0.3 * jax.random.normal(jax.random.fold_in(_rk, 611), (8, 128, 128), jnp.float32))
        _validS = jnp.arange(128)[None, :] < _lenS[:, None]
        _validS2 = jnp.arange(128)[None, :] < _lenS2[:, None]
        _causal = jnp.tril(jnp.ones((128, 128), dtype=bool))
        mask_BxS2_if1 = jnp.where(jnp.ones((8, 128), dtype=bool), 1, 0).astype(jnp.int32)
        return (x, ctx_1024, mask_BxS2_if1)
    x, ctx_1024, mask_BxS2_if1 = _rec_inputs()

    def _L0_attn_setup():
        import jax, jax.numpy as jnp
        import numpy as np
        N_HEADS = 16

        def _rope_tables(seq_len, head_dim, dtype):
            inv_freq = 1.0 / 10000.0 ** (jnp.arange(0, head_dim, 2, dtype=jnp.float32) / head_dim)
            t = jnp.arange(seq_len, dtype=jnp.float32)
            freqs = t[:, None] * inv_freq[None, :]
            return (jnp.cos(freqs).astype(dtype), jnp.sin(freqs).astype(dtype))

        def _apply_rope(x, cos, sin):
            d = x.shape[-1]
            x1, x2 = (x[..., :d // 2], x[..., d // 2:])
            return jnp.concatenate([x1 * cos - x2 * sin, x1 * sin + x2 * cos], axis=-1)
        key = jax.random.key(seed)
        k1, k2, k3, k4 = jax.random.split(key, 4)
        B, N, C = (2, 256, 128)
        x = jax.random.normal(k1, (B, N, C), dtype=jnp.float32)
        w_qkv = jax.random.normal(k2, (C, 3 * C), dtype=jnp.float32) * C ** (-0.5)
        w_proj = jax.random.normal(k3, (C, C), dtype=jnp.float32) * C ** (-0.5)
        b_proj = jax.random.normal(k4, (C,), dtype=jnp.float32) * 0.02
        return {'x': x, 'w_qkv': w_qkv, 'w_proj': w_proj, 'b_proj': b_proj}
    _L0_attn_all = _L0_attn_setup()
    _L0_attn_in = {k: v for k, v in _L0_attn_all.items() if k in ('w_qkv', 'w_proj', 'b_proj')}
    del _L0_attn_all

    def _L0_xattn_setup():
        import jax, jax.numpy as jnp
        import numpy as np
        D_MODEL = 128
        N_HEADS = 16
        B, S = (2, 256)
        key = jax.random.key(seed)
        ks = jax.random.split(key, 7)
        scale = 1.0 / np.sqrt(D_MODEL)
        return {'x_query': jax.random.normal(ks[0], (B, S, D_MODEL), dtype=jnp.float32), 'x_key': jax.random.normal(ks[1], (B, S, D_MODEL), dtype=jnp.float32), 'x_value': jax.random.normal(ks[2], (B, S, D_MODEL), dtype=jnp.float32), 'attention_mask': jnp.ones((B, S), dtype=jnp.int32), 'Wq': jax.random.normal(ks[3], (D_MODEL, D_MODEL), dtype=jnp.float32) * scale, 'Wk': jax.random.normal(ks[4], (D_MODEL, D_MODEL), dtype=jnp.float32) * scale, 'Wv': jax.random.normal(ks[5], (D_MODEL, D_MODEL), dtype=jnp.float32) * scale, 'Wo': jax.random.normal(ks[6], (D_MODEL, D_MODEL), dtype=jnp.float32) * scale}
    _L0_xattn_all = _L0_xattn_setup()
    _L0_xattn_in = {k: v for k, v in _L0_xattn_all.items() if k in ('Wq', 'Wk', 'Wv', 'Wo')}
    del _L0_xattn_all

    def _L0_ffn_setup():
        import jax, jax.numpy as jnp
        import numpy as np
        B, S, D = (4, 256, 128)
        E, H, TOP_K = (8, 256, 2)
        key = jax.random.key(seed)
        k_x, k_g, k_w1, k_w2, k_w3 = jax.random.split(key, 5)
        s_d = 1.0 / np.sqrt(D)
        s_h = 1.0 / np.sqrt(H)
        return {'x': jax.random.normal(k_x, (B, S, D), dtype=jnp.float32), 'w_gate': jax.random.normal(k_g, (D, E), dtype=jnp.float32) * s_d, 'w1': jax.random.normal(k_w1, (E, D, H), dtype=jnp.float32) * s_d, 'w3': jax.random.normal(k_w3, (E, D, H), dtype=jnp.float32) * s_d, 'w2': jax.random.normal(k_w2, (E, H, D), dtype=jnp.float32) * s_h}
    _L0_ffn_all = _L0_ffn_setup()
    _L0_ffn_in = {k: v for k, v in _L0_ffn_all.items() if k in ('w_gate', 'w1', 'w3', 'w2')}
    del _L0_ffn_all
    return {'x': x, 'ctx_1024': ctx_1024, 'mask_BxS2_if1': mask_BxS2_if1, 'L0_attn_w_qkv': _L0_attn_in['w_qkv'], 'L0_attn_w_proj': _L0_attn_in['w_proj'], 'L0_attn_b_proj': _L0_attn_in['b_proj'], 'L0_xattn_Wq': _L0_xattn_in['Wq'], 'L0_xattn_Wk': _L0_xattn_in['Wk'], 'L0_xattn_Wv': _L0_xattn_in['Wv'], 'L0_xattn_Wo': _L0_xattn_in['Wo'], 'L0_ffn_w_gate': _L0_ffn_in['w_gate'], 'L0_ffn_w1': _L0_ffn_in['w1'], 'L0_ffn_w3': _L0_ffn_in['w3'], 'L0_ffn_w2': _L0_ffn_in['w2']}

def reference(x, ctx_1024, mask_BxS2_if1, L0_attn_w_qkv, L0_attn_w_proj, L0_attn_b_proj, L0_xattn_Wq, L0_xattn_Wk, L0_xattn_Wv, L0_xattn_Wo, L0_ffn_w_gate, L0_ffn_w1, L0_ffn_w3, L0_ffn_w2):
    import jax
    import jax.numpy as jnp

    def _L0_attn_ref(x, w_qkv, w_proj, b_proj):
        import jax, jax.numpy as jnp
        import numpy as np
        N_HEADS = 16

        def _rope_tables(seq_len, head_dim, dtype):
            inv_freq = 1.0 / 10000.0 ** (jnp.arange(0, head_dim, 2, dtype=jnp.float32) / head_dim)
            t = jnp.arange(seq_len, dtype=jnp.float32)
            freqs = t[:, None] * inv_freq[None, :]
            return (jnp.cos(freqs).astype(dtype), jnp.sin(freqs).astype(dtype))

        def _apply_rope(x, cos, sin):
            d = x.shape[-1]
            x1, x2 = (x[..., :d // 2], x[..., d // 2:])
            return jnp.concatenate([x1 * cos - x2 * sin, x1 * sin + x2 * cos], axis=-1)
        B, N, C = x.shape
        H = N_HEADS
        d = C // H
        scale = d ** (-0.5)
        qkv = (x @ w_qkv).reshape(B, N, 3, H, d)
        qkv = jnp.transpose(qkv, (2, 0, 3, 1, 4))
        q, k, v = (qkv[0], qkv[1], qkv[2])
        cos, sin = _rope_tables(N, d, x.dtype)
        q = _apply_rope(q, cos, sin)
        k = _apply_rope(k, cos, sin)
        attn = jnp.einsum('bhqd,bhkd->bhqk', q, k) * scale
        attn = jax.nn.softmax(attn, axis=-1)
        out = jnp.einsum('bhqk,bhkd->bhqd', attn, v)
        out = jnp.transpose(out, (0, 2, 1, 3)).reshape(B, N, C)
        return out @ w_proj + b_proj

    def _L0_xattn_ref(x_query, x_key, x_value, attention_mask, Wq, Wk, Wv, Wo):
        import jax, jax.numpy as jnp
        import numpy as np
        D_MODEL = 128
        N_HEADS = 16
        B, S = (2, 256)
        b, sq, d = x_query.shape
        sk = x_key.shape[1]
        h = N_HEADS
        dk = d // h
        Q = (x_query @ Wq.T).reshape(b, sq, h, dk).transpose(0, 2, 1, 3)
        K = (x_key @ Wk.T).reshape(b, sk, h, dk).transpose(0, 2, 1, 3)
        V = (x_value @ Wv.T).reshape(b, sk, h, dk).transpose(0, 2, 1, 3)
        scores = jnp.einsum('bhqd,bhkd->bhqk', Q, K) / jnp.sqrt(jnp.asarray(dk, (scores_dtype := Q.dtype)))
        causal = jnp.tril(jnp.ones((sq, sk), dtype=bool))
        scores = jnp.where(causal[None, None, :, :], scores, -jnp.inf)
        pad = (attention_mask != 0)[:, None, None, :]
        scores = jnp.where(pad, scores, -jnp.inf)
        probs = jax.nn.softmax(scores, axis=-1)
        out = jnp.einsum('bhqk,bhkd->bhqd', probs, V)
        out = out.transpose(0, 2, 1, 3).reshape(b, sq, d)
        return out @ Wo.T

    def _L0_ffn_ref(x, w_gate, w1, w3, w2):
        import jax, jax.numpy as jnp
        import numpy as np
        B, S, D = (4, 256, 128)
        E, H, TOP_K = (8, 256, 2)
        bsz, seq_len, embed_dim = x.shape
        xt = x.reshape(-1, embed_dim)
        T = xt.shape[0]
        logits = xt @ w_gate
        top_logits, sel = jax.lax.top_k(logits, TOP_K)
        probs = jax.nn.softmax(top_logits, axis=-1).astype(x.dtype)
        h = jax.nn.silu(jnp.einsum('td,edh->eth', xt, w1)) * jnp.einsum('td,edh->eth', xt, w3)
        y = jnp.einsum('eth,ehd->etd', h, w2)
        t_idx = jnp.arange(T)
        yk = y[sel.T, t_idx[None, :], :]
        out = jnp.einsum('ktd,tk->td', yk, probs)
        return out.reshape(bsz, seq_len, embed_dim)
    x = x + _L0_attn_ref(_layernorm(x, axis=-1), L0_attn_w_qkv, L0_attn_w_proj, L0_attn_b_proj)
    x = x + _L0_xattn_ref(_layernorm(x, axis=-1), ctx_1024, ctx_1024, mask_BxS2_if1, L0_xattn_Wq, L0_xattn_Wk, L0_xattn_Wv, L0_xattn_Wo)
    x = x + _L0_ffn_ref(_layernorm(x, axis=-1), L0_ffn_w_gate, L0_ffn_w1, L0_ffn_w3, L0_ffn_w2)
    return x

_drawn_inputs = setup_inputs


def setup_inputs(seed=0):
    import zlib

    import numpy as np

    out = dict(_drawn_inputs(seed))
    spreads = {}
    factors = {}
    for name, (base, spread) in spreads.items():
        noise = np.random.default_rng([zlib.crc32(name.encode()), seed]).standard_normal(out[name].shape)
        drawn = base * np.exp(spread * noise) if base else spread * noise
        out[name] = jnp.asarray(drawn.astype(out[name].dtype))
    for name, factor in factors.items():
        out[name] = (out[name] * factor).astype(out[name].dtype)
    return out
```

```python
from contextlib import ExitStack

import concourse.bass as bass
from concourse import mybir

ALU = mybir.AluOpType
ACT = mybir.ActivationFunctionType
AX = mybir.AxisListType
F32 = mybir.dt.float32
BF16 = mybir.dt.bfloat16
I32 = mybir.dt.int32
U32 = mybir.dt.uint32

P = 128
NB = 8
NH = 16
DH = P // NH
GH = 4
NU = NH // GH
NA = 2 * NB
UNITS = NA * NU
LEAD_UNITS = 7
LEAD_PREP = 5
PR = 3
NE = 8
NHID = 256
NC = NHID // P
HB = NB // 2
ROWS = 96
PAD_ROW = 48
SHIFT_ROW = 64
BIG = 1e30
EPS = 1e-5
SCALE = float(DH) ** -0.5
C_ID, C_CAUSAL, C_COS, C_SIN, C_IOTA, C_HALF = 0, P, 2 * P, 3 * P, 4 * P, 4 * P + NE
NCONST = 4 * P + 2 * NE


def decoder_block(nc, x, ctx_in, mask, w_qkv, w_proj, b_proj, wq, wk, wv, wo, w_gate, w1, w3, w2, const, out):
    with ExitStack() as stack:
        def sb(name, shape, dt):
            return stack.enter_context(nc.sbuf_tensor(name, shape, dt))

        def psum(name):
            return stack.enter_context(nc.psum_tensor(name, [P, 512], F32))

        def sem(name):
            return stack.enter_context(nc.semaphore(name))

        bank_a = [psum("bank_a0"), psum("bank_a1")]
        bank_b = [psum("bank_b0"), psum("bank_b1")]
        bank_r = [psum("bank_r0"), psum("bank_r1")]
        bank_m = psum("bank_m")
        bank_n = psum("bank_n")

        consts = sb("consts", [P, NCONST], F32)
        ident = consts[:, C_ID:C_ID + P]
        causal_f = consts[:, C_CAUSAL:C_CAUSAL + P]
        cos_t = consts[:, C_COS:C_COS + P]
        sin_t = consts[:, C_SIN:C_SIN + P]
        iota = consts[:, C_IOTA:C_IOTA + NE]
        minus_half = consts[:, C_HALF:C_HALF + NE]
        ident_h = sb("ident_h", [P, P], BF16)
        causal_h = sb("causal_h", [P, P], BF16)
        one_rows = sb("one_rows", [2, NH * P], BF16)
        zero_rows = sb("zero_rows", [2, NH * P], BF16)
        mask_i = sb("mask_i", [NB, P], I32)
        pad_rows = sb("pad_rows", [NB, P], BF16)

        wqkv_sb = sb("wqkv_sb", [P, 3 * P], F32)
        wswap = sb("wswap", [P, 2 * P], F32)
        wproj_sb = sb("wproj_sb", [P, P], F32)
        bias_sb = sb("bias_sb", [P, P], F32)
        wx_sb = sb("wx_sb", [P, 4, P], F32)
        wxT = sb("wxT", [P, 4, P], F32)
        gate_sb = sb("gate_sb", [P, NE], F32)
        w1_sb = sb("w1_sb", [P, NE, NHID], F32)
        w3_sb = sb("w3_sb", [P, NE, NHID], F32)
        w2_sb = sb("w2_sb", [P, NE, NC, P], F32)

        res = sb("res", [P, NB, P], F32)
        ctx_sb = sb("ctx_sb", [P, NB, P], F32)
        stats = sb("stats", [P, 3 * NB, 6], F32)
        mv = sb("mv", [P, 3 * NB, 2], F32)
        veps = sb("veps", [P, 3 * NB], F32)
        rstd = sb("rstd", [P, 3 * NB], F32)
        xn1 = sb("xn1", [P, NB, P], F32)
        xn = sb("xn", [P, 2, P], F32)
        x1T = sb("x1T", [P, NB, P], F32)
        x2T = sb("x2T", [P, 2, P], F32)
        x3T = sb("x3T", [P, NB, P], F32)
        ctxT = sb("ctxT", [P, 2, P], F32)

        rot = sb("rot", [P, 2, 2, P], F32)
        rot_sw = sb("rot_sw", [P, 2, 2, P], F32)
        qk_f = sb("qk_f", [P, 2, 2, P], F32)
        rest = sb("rest", [P, 2, 2, P], F32)
        parts = sb("parts", [P, 2, 3, 2, P], BF16)
        rest_x = sb("rest_x", [P, 2, 2, P], F32)
        parts_x = sb("parts_x", [P, 2, 3, 2, P], BF16)
        qk_rows = sb("qk_rows", [ROWS, NB, 2, NH, P], BF16)
        v_aug = sb("v_aug", [P, NB, NH, 32], F32)
        neg_max = sb("neg_max", [P, 2, NH], F32)
        neg_max_h = sb("neg_max_h", [P, 2, 2, NH], BF16)
        shift = sb("shift", [2 * NH, 2, P], BF16)
        nan_fix = sb("nan_fix", [P, 4, NH], F32)
        probs = sb("probs", [P, PR, GH * P], F32)
        r_sb = sb("r_sb", [P, GH * P], F32)
        rden = sb("rden", [P, NH], F32)
        attn_o = sb("attn_o", [P, P], F32)
        attn_oT = sb("attn_oT", [P, P], F32)

        logits = sb("logits", [P, NB, NE], F32)
        top = sb("top", [P, NB, 8], F32)
        top_i = sb("top_i", [P, NB, 8], U32)
        top_f = sb("top_f", [P, NB, 2], F32)
        gap = sb("gap", [P, NB], F32)
        e_gap = sb("e_gap", [P, NB], F32)
        gden = sb("gden", [P, NB], F32)
        prob1 = sb("prob1", [P, NB], F32)
        prob2 = sb("prob2", [P, NB], F32)
        pick1 = sb("pick1", [P, NB, NE], F32)
        pick2 = sb("pick2", [P, NB, NE], F32)
        gates = sb("gates", [P, NB, NE], F32)
        silu_sb = sb("silu_sb", [P, NC, 512], F32)
        hid = sb("hid", [P, 2, NC, 512], F32)

        scratch = nc.dram_tensor("scratch", (NA, 2, 3, DH, NH, P), BF16, kind="Internal").ap()

        in_const, in_mask, in_wqkv, in_ctx = sem("in_const"), sem("in_mask"), sem("in_wqkv"), sem("in_ctx")
        in_wx, in_proj, in_gate, in_w13, in_w2 = sem("in_wx"), sem("in_proj"), sem("in_gate"), sem("in_w13"), sem("in_w2")
        in_x = [sem("in_x0"), sem("in_x1")]
        const_h = sem("const_h")
        rows_zero = [sem(f"rows_zero{b}") for b in range(NB)]
        rows_one = [sem(f"rows_one{b}") for b in range(NB)]
        v_zero, v_one = sem("v_zero"), sem("v_one")
        w_swapped, wxT_ready, wxT_taken = sem("w_swapped"), sem("wxT_ready"), sem("wxT_taken")
        stats_done, rstd_done, veps_done = sem("stats_done"), sem("rstd_done"), sem("veps_done")
        xn1_done, xn_done, bias_added = sem("xn1_done"), sem("xn_done"), sem("bias_added")
        x1T_ready, x1T_taken = sem("x1T_ready"), sem("x1T_taken")
        qkv_ready, rope_done, v_ready, v_taken = sem("qkv_ready"), sem("rope_done"), sem("v_ready"), sem("v_taken")
        sum_done, hi_done, rest_done, mid_done, lo_done = (sem("sum_done"), sem("hi_done"), sem("rest_done"),
                                                           sem("mid_done"), sem("lo_done"))
        ctxT_ready, ctxT_taken = sem("ctxT_ready"), sem("ctxT_taken")
        qkvx_ready, hix_done, vx_taken = sem("qkvx_ready"), sem("hix_done"), sem("vx_taken")
        restx_done, midx_done, lox_done = sem("restx_done"), sem("midx_done"), sem("lox_done")
        written = [sem(f"written{n}") for n in range(NA)]
        stacked = [sem(f"stacked{n}") for n in range(NA)]
        shifted = [sem(f"shifted{n}") for n in range(NA)]
        sa_ready, max_done = sem("sa_ready"), sem("max_done")
        nmh_done, nmT_ready, nmT_taken, nan_done = sem("nmh_done"), sem("nmT_ready"), sem("nmT_taken"), sem("nan_done")
        sb_ready, exp_done, masked, pv_done = sem("sb_ready"), sem("exp_done"), sem("masked"), sem("pv_done")
        r_taken, rT_ready, norm_done = sem("r_taken"), sem("rT_ready"), sem("norm_done")
        oT_ready, oT_taken, proj_ready, res_done = sem("oT_ready"), sem("oT_taken"), sem("proj_ready"), sem("res_done")
        xT_ready, xT_taken = sem("xT_ready"), sem("xT_taken")
        gate_ready, logits_taken, gap_done, e_gap_done, gates_done = (
            sem("gate_ready"), sem("logits_taken"), sem("gap_done"), sem("e_gap_done"), sem("gates_done"))
        up_ready, silu_done, hid_done, down_ready, y_taken = (
            sem("up_ready"), sem("silu_done"), sem("hid_done"), sem("down_ready"), sem("y_taken"))
        out_done = sem("out_done")

        CHUNKS = 2 * NE
        items = []
        for k in range(CHUNKS + 1):
            if k < CHUNKS:
                items += [("up", k, c) for c in range(NC)]
            if k >= 1:
                items.append(("down", k - 1, 0))
        TAIL = NA + 2
        tail_steps = [(n, g) for n in range(NA, TAIL) for g in range(NU)]

        def items_behind(n, g):
            if (n, g) not in tail_steps:
                return []
            at = tail_steps.index((n, g))
            return items[at:at + 1] if at < len(tail_steps) - 1 else items[at:]

        block = stack.enter_context(nc.Block())

        @block.sync
        def _(sp):
            for half in range(2):
                sp.dma_start(res[:, half * HB:(half + 1) * HB, :],
                             x[half * HB:(half + 1) * HB].rearrange("b t c -> t b c")).then_inc(in_x[half], 16)
                if half == 0:
                    sp.dma_start(consts[:], const).then_inc(in_const, 16)
                    sp.dma_start(wqkv_sb[:], w_qkv).then_inc(in_wqkv, 16)
            sp.dma_start(mask_i[:], mask).then_inc(in_mask, 16)
            for i, w in enumerate((wq, wk, wv, wo)):
                sp.dma_start(wx_sb[:, i, :], w).then_inc(in_wx, 16)
            sp.dma_start(ctx_sb[:], ctx_in.rearrange("b t c -> t b c")).then_inc(in_ctx, 16)
            sp.dma_start(wproj_sb[:], w_proj).then_inc(in_proj, 16)
            sp.dma_start(bias_sb[:], b_proj.rearrange("(o c) -> o c", o=1).to_broadcast([P, P])).then_inc(in_proj, 16)
            sp.dma_start(gate_sb[:], w_gate).then_inc(in_gate, 16)

            def rows_of_ones(b):
                sp.wait_ge(const_h, 1)
                sp.wait_ge(rows_zero[b], 1)
                sp.dma_start(qk_rows[PAD_ROW:PAD_ROW + 1, b, 0, :, :], one_rows[0:1, :]).then_inc(rows_one[b], 16)
                sp.dma_start(qk_rows[SHIFT_ROW:SHIFT_ROW + 2, b, 1, :, :], one_rows[:]).then_inc(rows_one[b], 16)

            def write_parts(n, tile):
                for t in range(2):
                    for part in range(3):
                        sp.dma_start(scratch[n, t, part].rearrange("d h t -> h d t"),
                                     tile[:, part, t, :]).then_inc(written[n], 16)

            def read_rows(n):
                b = n % NB
                sp.wait_ge(written[n], 6 * 16)
                for r, part, copies in ((0, 0, 3), (24, 1, 2), (40, 2, 1)):
                    sp.dma_start(qk_rows[r:r + copies * DH, b, 0, :, :],
                                 scratch[n, 0, part:part + 1].to_broadcast([copies, DH, NH, P]))\
                        .then_inc(stacked[n], 16)
                for r, count in ((0, 3), (24, 2), (40, 1)):
                    sp.dma_start(qk_rows[r:r + count * DH, b, 1, :, :],
                                 scratch[n, 1, 0:count].rearrange("p d h t -> (p d) h t")).then_inc(stacked[n], 16)

            def prep_self(p):
                sp.wait_ge(lo_done, p + 1)
                write_parts(p, parts[:, p % 2])
                rows_of_ones(p)
                read_rows(p)

            def prep_cross(b):
                sp.wait_ge(lox_done, b + 1)
                write_parts(NB + b, parts_x[:, b % 2])
                sp.wait_ge(sb_ready, NU * (b + 1))
                sp.dma_start(qk_rows[SHIFT_ROW:SHIFT_ROW + 2, b, 0, :, :], zero_rows[:]).then_inc(stacked[NB + b], 16)
                sp.dma_start(qk_rows[PAD_ROW:PAD_ROW + 1, b, 1, :, :],
                             pad_rows[b:b + 1, :].unsqueeze(1).to_broadcast([1, NH, P])).then_inc(stacked[NB + b], 16)
                read_rows(NB + b)

            def put_shift(n):
                sp.wait_ge(nmT_taken, n + 1)
                sp.wait_ge(sa_ready, NU * (n + 1))
                sp.dma_start(qk_rows[SHIFT_ROW:SHIFT_ROW + 2, n % NB, 0, :, :], shift[:, n % 2, :])\
                    .then_inc(shifted[n], 16)

            for p in range(2):
                prep_self(p)
            sp.dma_start(w1_sb[:], w1.rearrange("e d h -> d e h")).then_inc(in_w13, 16)
            sp.dma_start(w3_sb[:], w3.rearrange("e d h -> d e h")).then_inc(in_w13, 16)
            sp.dma_start(w2_sb[:], w2.rearrange("e (c p) d -> p e c d", p=P)).then_inc(in_w2, 16)
            prep_self(2)
            put_shift(0)
            prep_self(3)
            prep_self(4)
            for n in range(NA):
                if n + 1 < NA:
                    put_shift(n + 1)
                if LEAD_PREP <= n - 1 + LEAD_PREP < NB and n >= 1:
                    prep_self(n - 1 + LEAD_PREP)
                if 0 <= n - 3 < NB:
                    prep_cross(n - 3)
            for half in range(2):
                sp.wait_ge(y_taken, NE * (half + 1))
                sp.dma_start(out[half * HB:(half + 1) * HB].rearrange("b t c -> t b c"),
                             res[:, half * HB:(half + 1) * HB, :]).then_inc(out_done, 16)
            sp.wait_ge(out_done, 32)

        @block.tensor
        def _(pe):
            def transpose_x1(p, bank):
                pe.wait_ge(xn1_done, p + 1)
                pe.transpose(bank[:, 0:P], xn1[:, p, :], ident).then_inc(x1T_ready, 1)

            def project_qk(p, bank):
                pe.wait_ge(x1T_taken, p + 1)
                for i, w in enumerate((wqkv_sb[:, 0:P], wqkv_sb[:, P:2 * P], wswap[:, 0:P], wswap[:, P:2 * P])):
                    mm = pe.matmul(bank[:, i * P:(i + 1) * P], w, x1T[:, p, :], start=True, stop=True)
                mm.then_inc(qkv_ready, 1)

            def project_v(p, bank):
                pe.wait_ge(x1T_taken, p + 1)
                pe.matmul(bank[:, 3 * P:4 * P], x1T[:, p, :], wqkv_sb[:, 2 * P:3 * P],
                          start=True, stop=True).then_inc(v_ready, 1)

            def scores_a(u):
                n, g = divmod(u, NU)
                b = n % NB
                if g == 0:
                    pe.wait_ge(stacked[n], (6 if n < NB else 8) * 16)
                    pe.wait_ge(rows_one[b], 32)
                if u < 2:
                    pe.wait_ge(x1T_taken, LEAD_PREP)
                else:
                    pe.wait_ge(max_done, u - 1)
                bank = bank_a[u % 2]
                for j in range(GH):
                    h = g * GH + j
                    mm = pe.matmul(bank[:, j * P:(j + 1) * P], qk_rows[:, b, 0, h, :], qk_rows[:, b, 1, h, :],
                                   start=(n < NB or j == 0), stop=(n < NB), skip_group_check=True)
                if n >= NB:
                    mm = pe.matmul(bank[:, :], ident_h[:], causal_h[:].unsqueeze(1).to_broadcast([P, GH, P]),
                                   start=False, stop=True, skip_group_check=True)
                mm.then_inc(sa_ready, 1)

            def scores_b(u):
                n, g = divmod(u, NU)
                b = n % NB
                if g == 0:
                    pe.wait_ge(shifted[n], 16)
                if u < 2:
                    pe.wait_ge(rope_done, LEAD_PREP)
                else:
                    pe.wait_ge(exp_done, u - 1)
                for j in range(GH):
                    h = g * GH + j
                    mm = pe.matmul(bank_b[u % 2][:, j * P:(j + 1) * P], qk_rows[:, b, 1, h, :],
                                   qk_rows[:, b, 0, h, :], start=True, stop=True)
                mm.then_inc(sb_ready, 1)

            def product_v(u):
                n, g = divmod(u, NU)
                if g == 0:
                    if n == 0:
                        pe.wait_ge(v_one, 1)
                    if n < NB:
                        pe.wait_ge(v_taken, max(n + 1, LEAD_PREP))
                    else:
                        pe.wait_ge(vx_taken, n - NB + 1)
                    if n >= 2:
                        pe.wait_ge(r_taken, n - 1)
                if n < NB:
                    pe.wait_ge(exp_done, u + 1)
                else:
                    pe.wait_ge(masked, u - NB * NU + 1)
                for j in range(GH):
                    mm = pe.matmul(bank_r[n % 2][32 * j:32 * j + 32, g * P:(g + 1) * P],
                                   v_aug[:, n % NB, g * GH + j, :], probs[:, u % PR, j * P:(j + 1) * P],
                                   start=True, stop=True)
                mm.then_inc(pv_done, 1)

            def max_transpose(n):
                pe.wait_ge(nmh_done, n + 1)
                if n == 0:
                    pe.wait_ge(const_h, 1)
                pe.transpose(bank_n[0:2 * NH, 0:P // 2].bitcast(BF16),
                             neg_max_h[:, n % 2, :, :].rearrange("p a h -> p (a h)"), ident_h[:]).then_inc(nmT_ready, 1)

            def up(k, c):
                half, e = divmod(k, NE)
                if k == 0 and c == 0:
                    pe.wait_ge(in_w13, 32)
                    pe.wait_ge(max_done, UNITS)
                    pe.wait_ge(exp_done, UNITS)
                if k >= 1:
                    pe.wait_ge(silu_done, NC * (k - 1) + c + 1)
                    pe.wait_ge(hid_done, NC * (k - 1) + c + 1)
                if e == 0 and c == 0:
                    pe.wait_ge(xT_taken, NB + HB * (half + 1))
                rhs = x3T[:, half * HB:(half + 1) * HB, :].rearrange("p b t -> p (b t)")
                pe.matmul(bank_a[c][:, :], w1_sb[:, e, c * P:(c + 1) * P], rhs, start=True, stop=True)
                pe.matmul(bank_b[c][:, :], w3_sb[:, e, c * P:(c + 1) * P], rhs, start=True, stop=True)\
                    .then_inc(up_ready, 1)

            def down(k):
                if k == 0:
                    pe.wait_ge(in_w2, 16)
                    pe.wait_ge(r_taken, NA)
                if k >= 2:
                    pe.wait_ge(y_taken, k - 1)
                pe.wait_ge(hid_done, NC * (k + 1))
                for bb in range(HB):
                    for c in range(NC):
                        mm = pe.matmul(bank_r[k % 2][:, bb * P:(bb + 1) * P], hid[:, k % 2, c, bb * P:(bb + 1) * P],
                                       w2_sb[:, k % NE, c, :], start=(c == 0), stop=(c == NC - 1))
                mm.then_inc(down_ready, 1)

            pe.wait_ge(in_const, 16)
            for p in range(LEAD_PREP):
                if p >= 2:
                    pe.wait_ge(x1T_taken, p - 1)
                transpose_x1(p, bank_a[p % 2])
                if p == 0:
                    pe.wait_ge(in_wqkv, 16)
                    pe.wait_ge(w_swapped, 1)
                if p >= 2:
                    pe.wait_ge(rope_done, p - 1)
                project_qk(p, bank_b[p % 2])
                if p >= 2:
                    pe.wait_ge(v_taken, p - 1)
                project_v(p, bank_r[p % 2])
            pe.wait_ge(in_wx, 64)
            for i in range(4):
                mm = pe.transpose(bank_m[:, i * P:(i + 1) * P], wx_sb[:, i, :], ident)
            mm.then_inc(wxT_ready, 1)
            for u in range(LEAD_UNITS):
                scores_a(u)
            max_transpose(0)

            for n in range(TAIL):
                for g in range(NU):
                    u = n * NU + g
                    if u + LEAD_UNITS < UNITS:
                        scores_a(u + LEAD_UNITS)
                    if u < UNITS:
                        scores_b(u)
                    if 1 <= u <= UNITS:
                        product_v(u - 1)
                    if g == 0:
                        if n + LEAD_PREP < NB or 0 <= n - 2 < NB:
                            if n == 0:
                                pe.wait_ge(wxT_taken, 1)
                            elif n >= 2:
                                pe.wait_ge(res_done, n - 1)
                        if n + LEAD_PREP < NB:
                            transpose_x1(n + LEAD_PREP, bank_m)
                        if 0 <= n - 2 < NB:
                            if n == 2:
                                pe.wait_ge(in_ctx, 16)
                            if n >= 4:
                                pe.wait_ge(qkvx_ready, n - 3)
                            pe.transpose(bank_m[:, P:2 * P], ctx_sb[:, n - 2, :], ident).then_inc(ctxT_ready, 1)
                    if g == 1:
                        if n + 1 < NA:
                            if n == 0:
                                pass
                            if n >= 1 and n - 1 + LEAD_PREP < NB:
                                pe.wait_ge(v_taken, n + LEAD_PREP)
                            if 0 <= n - 3 < NB:
                                pe.wait_ge(vx_taken, n - 2)
                                pe.wait_ge(restx_done, n - 2)
                            if n - 1 >= NB + 2:
                                pe.wait_ge(logits_taken, n - NB - 2)
                            max_transpose(n + 1)
                        if 1 <= n <= NA:
                            if n + LEAD_PREP < NB:
                                pe.wait_ge(x1T_taken, n + LEAD_PREP + 1)
                            if 0 <= n - 2 < NB:
                                pe.wait_ge(ctxT_taken, n - 1)
                            elif n >= 2:
                                pe.wait_ge(res_done, n - 1)
                            pe.wait_ge(r_taken, n)
                            for i in range(GH):
                                mm = pe.transpose(bank_m[:, i * P:(i + 1) * P], r_sb[:, i * P:(i + 1) * P], ident)
                            mm.then_inc(rT_ready, 1)
                    if g == 2:
                        if n + LEAD_PREP < NB:
                            pe.wait_ge(nmT_taken, n + 2)
                            project_qk(n + LEAD_PREP, bank_n)
                        if 1 <= n <= NA:
                            pe.wait_ge(norm_done, n)
                            pe.transpose(bank_m[:, 0:P], attn_o[:], ident).then_inc(oT_ready, 1)
                        if n >= 2:
                            if n > NA:
                                pe.wait_ge(res_done, n - 1)
                            pe.wait_ge(xn_done, n - 1)
                            pe.transpose(bank_m[:, P:2 * P], xn[:, n % 2, :], ident).then_inc(xT_ready, 1)
                    if g == 3:
                        if n + LEAD_PREP < NB:
                            pe.wait_ge(rope_done, n + LEAD_PREP + 1)
                            project_v(n + LEAD_PREP, bank_n)
                        elif n + 1 < NA:
                            pe.wait_ge(nmT_taken, n + 2)
                        if 0 <= n - 2 < NB:
                            m = n - 2
                            pe.wait_ge(xT_taken, m + 1)
                            pe.wait_ge(ctxT_taken, m + 1)
                            pe.matmul(bank_n[:, 0:P], wxT[:, 0, :], x2T[:, m % 2, :], start=True, stop=True)
                            pe.matmul(bank_n[:, P:2 * P], wxT[:, 1, :], ctxT[:, m % 2, :], start=True, stop=True)
                            pe.matmul(bank_n[:, 2 * P:3 * P], ctxT[:, m % 2, :], wxT[:, 2, :], start=True, stop=True)\
                                .then_inc(qkvx_ready, 1)
                        if n - 2 >= NB:
                            m = n - 2 - NB
                            if n == NB + 2:
                                pe.wait_ge(in_gate, 16)
                            if m >= 1:
                                pe.wait_ge(logits_taken, m)
                            pe.wait_ge(xT_taken, n - 1)
                            pe.matmul(bank_n[:, 0:NE], x3T[:, m, :], gate_sb[:], start=True, stop=True)\
                                .then_inc(gate_ready, 1)
                        if 1 <= n <= NA:
                            pe.wait_ge(oT_taken, n)
                            if n >= 2:
                                pe.wait_ge(xT_taken, n - 1)
                            if n == 1:
                                pe.wait_ge(in_proj, 32)
                            pe.matmul(bank_m[:, 0:P], attn_oT[:], wproj_sb[:] if n <= NB else wxT[:, 3, :],
                                      start=True, stop=True).then_inc(proj_ready, 1)
                    for kind, k, c in items_behind(n, g):
                        if kind == "up":
                            up(k, c)
                        else:
                            down(k)

        @block.scalar
        def _(act):
            def clear_rows(b):
                act.memzero(qk_rows[:, b].rearrange("p a h t -> p (a h t)")).then_inc(rows_zero[b], 1)

            def copy_x1T(p, bank):
                act.wait_ge(x1T_ready, p + 1)
                act.activation(x1T[:, p, :], bank[:, 0:P], ACT.Copy).then_inc(x1T_taken, 1)

            def copy_v(p, bank):
                act.wait_ge(v_ready, p + 1)
                act.activation(v_aug[:, p, :, 0:DH], bank[:, 3 * P:4 * P].rearrange("p (h d) -> p h d", h=NH), ACT.Copy)\
                    .then_inc(v_taken, 1)

            def hi_self(p):
                act.wait_ge(sum_done, p + 1)
                if p >= 2:
                    act.wait_ge(written[p - 2], 6 * 16)
                act.activation(parts[:, p % 2, 0], qk_f[:, p % 2], ACT.Copy).then_inc(hi_done, 1)

            def mid_self(p):
                act.wait_ge(rest_done, p + 1)
                act.activation(parts[:, p % 2, 1], rest[:, p % 2], ACT.Copy).then_inc(mid_done, 1)

            def hi_cross(m):
                act.wait_ge(qkvx_ready, m + 1)
                act.wait_ge(pv_done, NU * (m + 1))
                act.activation(v_aug[:, m, :, 0:DH], bank_n[:, 2 * P:3 * P].rearrange("p (h d) -> p h d", h=NH), ACT.Copy)\
                    .then_inc(vx_taken, 1)
                if m >= 2:
                    act.wait_ge(written[NB + m - 2], 6 * 16)
                act.activation(parts_x[:, m % 2, 0], bank_n[:, 0:2 * P].rearrange("p (a t) -> p a t", a=2), ACT.Copy)\
                    .then_inc(hix_done, 1)

            def mid_cross(m):
                act.wait_ge(restx_done, m + 1)
                act.activation(parts_x[:, m % 2, 1], rest_x[:, m % 2], ACT.Copy).then_inc(midx_done, 1)

            def silu(k, c):
                act.wait_ge(up_ready, NC * k + c + 1)
                if k >= 1:
                    act.wait_ge(hid_done, NC * (k - 1) + c + 1)
                act.activation(silu_sb[:, c, :], bank_a[c][:, :], ACT.Silu).then_inc(silu_done, 1)

            act.memzero(v_aug[:].rearrange("p b h c -> p (b h c)")).then_inc(v_zero, 1)
            clear_rows(1)
            act.wait_ge(v_zero, 1)
            for p in range(LEAD_PREP):
                copy_x1T(p, bank_a[p % 2])
                copy_v(p, bank_r[p % 2])
                if p == 0:
                    clear_rows(3)
                hi_self(p)
                mid_self(p)
            act.wait_ge(wxT_ready, 1)
            act.activation(wxT[:], bank_m[:, :].rearrange("p (a t) -> p a t", a=4), ACT.Copy).then_inc(wxT_taken, 1)

            for n in range(TAIL):
                for g in range(NU):
                    u = n * NU + g
                    if u < UNITS:
                        act.wait_ge(sb_ready, u + 1)
                        if u >= PR:
                            act.wait_ge(pv_done, u - PR + 1)
                        act.activation(probs[:, u % PR, :], bank_b[u % 2][:, :], ACT.Exp, scale=SCALE)\
                            .then_inc(exp_done, 1)
                    if g == 0:
                        if 1 <= n <= NA:
                            act.wait_ge(pv_done, NU * n)
                            if n >= 2:
                                act.wait_ge(rT_ready, n - 1)
                            act.activation(r_sb[:], bank_r[(n - 1) % 2][:, :], ACT.Copy).then_inc(r_taken, 1)
                        if 0 <= n - 2 < NB:
                            act.wait_ge(ctxT_ready, n - 1)
                        if n + LEAD_PREP < NB:
                            copy_x1T(n + LEAD_PREP, bank_m)
                        if 0 <= n - 2 < NB:
                            act.activation(ctxT[:, n % 2, :], bank_m[:, P:2 * P], ACT.Copy).then_inc(ctxT_taken, 1)
                    if g == 1:
                        if 1 <= n and n - 1 + LEAD_PREP < NB:
                            mid_self(n - 1 + LEAD_PREP)
                        if 0 <= n - 3 < NB:
                            mid_cross(n - 3)
                    if g == 2:
                        if n >= 2:
                            act.wait_ge(xT_ready, n - 1)
                        if 1 <= n <= NA:
                            act.wait_ge(oT_ready, n)
                            if n >= 2:
                                act.wait_ge(proj_ready, n - 1)
                            act.activation(attn_oT[:], bank_m[:, 0:P], ACT.Copy).then_inc(oT_taken, 1)
                        if n >= 2:
                            m = n - 2
                            if 2 <= m < NB:
                                act.wait_ge(qkvx_ready, m - 1)
                            act.activation(x2T[:, m % 2, :] if m < NB else x3T[:, m - NB, :], bank_m[:, P:2 * P],
                                           ACT.Copy).then_inc(xT_taken, 1)
                    if g == 3:
                        if n + LEAD_PREP < NB:
                            hi_self(n + LEAD_PREP)
                            if n >= 2:
                                act.wait_ge(qkvx_ready, n - 1)
                            copy_v(n + LEAD_PREP, bank_n)
                        if 0 <= n - 2 < NB:
                            hi_cross(n - 2)
                        if n in (NB + 2 + HB - 1, TAIL - 1):
                            half = 0 if n < TAIL - 1 else 1
                            hs = slice(half * HB, (half + 1) * HB)
                            act.wait_ge(gap_done, half + 1)
                            act.activation(e_gap[:, hs], gap[:, hs], ACT.Exp).then_inc(e_gap_done, 1)
                    for kind, k, c in items_behind(n, g):
                        if kind == "up":
                            silu(k, c)

        @block.vector
        def _(dve):
            steps = [0]
            dve_step = sem("dve_step")

            def then(ins):
                steps[0] += 1
                ins.then_inc(dve_step, 1)
                dve.wait_ge(dve_step, steps[0])

            def norm_stats(src, slot):
                then(dve.bn_stats(stats[:, slot, :], src))
                dve.bn_aggr(mv[:, slot, :], stats[:, slot, :]).then_inc(stats_done, 1)

            def normalise(dst, src, slot, done):
                dve.tensor_scalar(dst, src, mv[:, slot, 0:1], rstd[:, slot:slot + 1], ALU.subtract, ALU.mult)\
                    .then_inc(done, 1)

            def maximum(u):
                n, g = divmod(u, NU)
                dve.wait_ge(sa_ready, u + 1)
                if g == 0 and n >= 2:
                    dve.wait_ge(nmh_done, n - 1)
                    if n >= NB + 2:
                        dve.wait_ge(nan_done, n - 1 - NB)
                dve.tensor_reduce(neg_max[:, n % 2, g * GH:(g + 1) * GH],
                                  bank_a[u % 2][:, :].rearrange("p (h k) -> p h k", h=GH), AX.X, ALU.max, negate=True)\
                    .then_inc(max_done, 1)

            def split_max(n):
                dve.wait_ge(max_done, NU * (n + 1))
                if n >= 2:
                    dve.wait_ge(nmT_ready, n - 1)
                then(dve.tensor_copy(neg_max_h[:, n % 2, 0, :], neg_max[:, n % 2, :]))
                dve.tensor_tensor(neg_max_h[:, n % 2, 1, :], neg_max[:, n % 2, :], neg_max_h[:, n % 2, 0, :],
                                  ALU.subtract).then_inc(nmh_done, 1)
                if n >= NB:
                    if n >= NB + 4:
                        dve.wait_ge(norm_done, n - 3)
                    dve.tensor_scalar(nan_fix[:, n % 4, :], neg_max[:, n % 2, :], 1e10, 0.0, ALU.mult, ALU.mult)\
                        .then_inc(nan_done, 1)

            def take_max(n):
                dve.wait_ge(nmT_ready, n + 1)
                if n >= 2:
                    dve.wait_ge(shifted[n - 2], 16)
                dve.tensor_copy(shift[:, n % 2, :], bank_n[0:2 * NH, 0:P // 2].bitcast(BF16)).then_inc(nmT_taken, 1)

            def rope(p, bank):
                dve.wait_ge(qkv_ready, p + 1)
                if p >= 2:
                    dve.wait_ge(sum_done, p - 1)
                v = bank[:, :].rearrange("p (a t) -> p a t", a=4)
                dve.tensor_tensor(rot[:, p % 2], v[:, 0:2, :], cos_t.unsqueeze(1).to_broadcast([P, 2, P]), ALU.mult)
                dve.tensor_tensor(rot_sw[:, p % 2], v[:, 2:4, :], sin_t.unsqueeze(1).to_broadcast([P, 2, P]), ALU.mult)\
                    .then_inc(rope_done, 1)

            def divide(n):
                dve.wait_ge(rT_ready, n + 1)
                v = bank_m[:, :].rearrange("p (h c) -> p h c", c=32)
                then(dve.reciprocal(rden[:], v[:, :, DH]))
                if n >= NB:
                    dve.wait_ge(nan_done, n - NB + 1)
                    then(dve.tensor_tensor(rden[:], rden[:], nan_fix[:, n % 4, :], ALU.add))
                if n >= 1:
                    dve.wait_ge(oT_ready, n)
                dve.tensor_tensor(attn_o[:].rearrange("p (h d) -> p h d", h=NH), v[:, :, 0:DH],
                                  rden[:].unsqueeze(2).to_broadcast([P, NH, DH]), ALU.mult).then_inc(norm_done, 1)

            def add_residual(n):
                b = n % NB
                dve.wait_ge(proj_ready, n + 1)
                if n % HB == 0 and n < NB:
                    dve.wait_ge(bias_added, n // HB + 1)
                if n >= NB:
                    dve.wait_ge(res_done, n - NB + 1)
                dve.tensor_tensor(res[:, b, :], bank_m[:, 0:P], res[:, b, :], ALU.add).then_inc(res_done, 1)
                dve.wait_ge(res_done, n + 1)
                norm_stats(res[:, b, :], NB + n)

            def gating(half):
                hs = slice(half * HB, (half + 1) * HB)
                wide = [P, HB, NE]
                for b in range(half * HB, (half + 1) * HB):
                    then(dve.max(out=top[:, b, :], in_=logits[:, b, :]))
                    then(dve.max_index(out=top_i[:, b, :], in_max=top[:, b, :], in_values=logits[:, b, :]))
                dve.tensor_tensor(gap[:, hs], top[:, hs, 1], top[:, hs, 0], ALU.subtract).then_inc(gap_done, 1)
                then(dve.tensor_copy(top_f[:, hs, :], top_i[:, hs, 0:2]))
                for i, pick in enumerate((pick1, pick2)):
                    then(dve.tensor_tensor(pick[:, hs, :], iota.unsqueeze(1).to_broadcast(wide),
                                           top_f[:, hs, i].unsqueeze(2).to_broadcast(wide), ALU.is_equal))
                dve.wait_ge(e_gap_done, half + 1)
                then(dve.tensor_scalar(gden[:, hs], e_gap[:, hs], 1.0, None, ALU.add))
                then(dve.reciprocal(prob1[:, hs], gden[:, hs]))
                then(dve.tensor_tensor(prob2[:, hs], e_gap[:, hs], prob1[:, hs], ALU.mult))
                then(dve.tensor_tensor(pick1[:, hs, :], pick1[:, hs, :], prob1[:, hs].unsqueeze(2).to_broadcast(wide), ALU.mult))
                then(dve.tensor_tensor(pick2[:, hs, :], pick2[:, hs, :], prob2[:, hs].unsqueeze(2).to_broadcast(wide), ALU.mult))
                dve.tensor_tensor(gates[:, hs, :], pick1[:, hs, :], pick2[:, hs, :], ALU.add).then_inc(gates_done, 1)

            def hidden(k, c):
                dve.wait_ge(silu_done, NC * k + c + 1)
                if k >= 2 and c == 0:
                    dve.wait_ge(down_ready, k - 1)
                dve.tensor_tensor(hid[:, k % 2, c, :], bank_b[c][:, :], silu_sb[:, c, :], ALU.mult).then_inc(hid_done, 1)

            def add_expert(k):
                half, e = divmod(k, NE)
                dve.wait_ge(down_ready, k + 1)
                if e == 0:
                    dve.wait_ge(gates_done, half + 1)
                    dve.wait_ge(res_done, NB + HB * (half + 1))
                if k >= 1:
                    dve.wait_ge(y_taken, k)
                for bb in range(HB):
                    b = half * HB + bb
                    ins = dve.scalar_tensor_tensor(out=res[:, b, :], in0=bank_r[k % 2][:, bb * P:(bb + 1) * P],
                                                   scalar=gates[:, b, e:e + 1], in1=res[:, b, :],
                                                   op0=ALU.mult, op1=ALU.add)
                ins.then_inc(y_taken, 1)

            dve.memset(one_rows[:], 1.0)
            dve.memset(zero_rows[:], 0.0)
            dve.memset(qk_rows[:, 0], 0.0).then_inc(rows_zero[0], 1)
            dve.wait_ge(in_x[0], 16)
            for b in range(HB):
                norm_stats(res[:, b, :], b)
            dve.wait_ge(in_const, 16)
            dve.wait_ge(in_wqkv, 16)
            src = wqkv_sb[:, 0:2 * P].rearrange("p (h s j) -> p h s j", s=2, j=DH // 2)
            dst = wswap[:].rearrange("p (h s j) -> p h s j", s=2, j=DH // 2)
            dve.tensor_copy(dst[:, :, 0, :], src[:, :, 1, :])
            dve.tensor_copy(dst[:, :, 1, :], src[:, :, 0, :]).then_inc(w_swapped, 1)
            dve.tensor_copy(ident_h[:], ident)
            dve.tensor_copy(causal_h[:], causal_f)
            dve.wait_ge(in_mask, 16)
            dve.tensor_scalar(pad_rows[:], mask_i[:], 0.0, -BIG, ALU.is_equal, ALU.mult).then_inc(const_h, 1)
            dve.wait_ge(rstd_done, 1)
            for b in range(HB):
                normalise(xn1[:, b, :], res[:, b, :], b, xn1_done)
            rope(0, bank_b[0])
            dve.wait_ge(v_zero, 1)
            dve.memset(v_aug[:, :, :, DH], 1.0).then_inc(v_one, 1)
            for b in range(1, HB):
                rope(b, bank_b[b % 2])
            dve.wait_ge(in_x[1], 16)
            for b in range(HB, NB):
                norm_stats(res[:, b, :], b)
            dve.wait_ge(rstd_done, 2)
            for b in range(HB, NB):
                normalise(xn1[:, b, :], res[:, b, :], b, xn1_done)
            for p in range(HB, LEAD_PREP):
                rope(p, bank_b[p % 2])
            for u in range(LEAD_UNITS):
                maximum(u)
                if u == NU - 1:
                    split_max(0)
            take_max(0)

            for n in range(TAIL):
                for g in range(NU):
                    u = n * NU + g
                    if u + LEAD_UNITS < UNITS:
                        maximum(u + LEAD_UNITS)
                    if g == 0:
                        if n + 1 < NA:
                            split_max(n + 1)
                        if n >= 2:
                            add_residual(n - 2)
                    if g == 1:
                        if n + 1 < NA:
                            take_max(n + 1)
                        if 1 <= n <= NA:
                            divide(n - 1)
                        if n >= 2:
                            dve.wait_ge(rstd_done, 2 + n - 1)
                            if n >= 4:
                                dve.wait_ge(xT_ready, n - 3)
                            normalise(xn[:, n % 2, :], res[:, (n - 2) % NB, :], NB + n - 2, xn_done)
                    if g == 2 and n + LEAD_PREP < NB:
                        rope(n + LEAD_PREP, bank_n)
                    if g == 3:
                        if 0 <= n - 2 < NB:
                            m = n - 2
                            dve.wait_ge(hix_done, m + 1)
                            if m >= 2:
                                dve.wait_ge(lox_done, m - 1)
                            dve.tensor_tensor(rest_x[:, m % 2], bank_n[:, 0:2 * P].rearrange("p (a t) -> p a t", a=2),
                                              parts_x[:, m % 2, 0], ALU.subtract).then_inc(restx_done, 1)
                        if n - 2 >= NB:
                            m = n - 2 - NB
                            dve.wait_ge(gate_ready, m + 1)
                            dve.tensor_copy(logits[:, m, :], bank_n[:, 0:NE]).then_inc(logits_taken, 1)
                            if m % HB == HB - 1:
                                dve.wait_ge(logits_taken, m + 1)
                                gating(m // HB)
                    for kind, k, c in items_behind(n, g):
                        if kind == "up":
                            hidden(k, c)
                        else:
                            add_expert(k)

        @block.gpsimd
        def _(pool):
            def clear_rows(b):
                pool.memset(qk_rows[:, b].bitcast(U32), 0).then_inc(rows_zero[b], 1)

            def inverse_std(slots, count):
                pool.wait_ge(stats_done, slots.stop)
                pool.tensor_scalar(veps[:, slots], mv[:, slots, 1], EPS, 1.0, ALU.add, ALU.mult).then_inc(veps_done, 1)
                pool.wait_ge(veps_done, count)
                pool.tensor_tensor(rstd[:, slots], veps[:, slots], minus_half[:, 0:slots.stop - slots.start], ALU.pow)\
                    .then_inc(rstd_done, 1)

            def sum_self(p):
                pool.wait_ge(rope_done, p + 1)
                if p >= 2:
                    pool.wait_ge(hi_done, p - 1)
                    pool.wait_ge(rest_done, p - 1)
                pool.tensor_tensor(qk_f[:, p % 2], rot[:, p % 2], rot_sw[:, p % 2], ALU.add).then_inc(sum_done, 1)

            def rest_self(p):
                pool.wait_ge(sum_done, p + 1)
                pool.wait_ge(hi_done, p + 1)
                if p >= 2:
                    pool.wait_ge(lo_done, p - 1)
                pool.tensor_tensor(rest[:, p % 2], qk_f[:, p % 2], parts[:, p % 2, 0], ALU.subtract).then_inc(rest_done, 1)

            def lo_self(p):
                pool.wait_ge(rest_done, p + 1)
                pool.wait_ge(mid_done, p + 1)
                pool.tensor_tensor(parts[:, p % 2, 2], rest[:, p % 2], parts[:, p % 2, 1], ALU.subtract).then_inc(lo_done, 1)

            clear_rows(2)
            pool.wait_ge(in_const, 16)
            inverse_std(slice(0, HB), 1)
            for p in range(LEAD_PREP):
                if p == HB:
                    inverse_std(slice(HB, NB), 2)
                    pool.wait_ge(in_proj, 32)
                    for half in range(2):
                        pool.wait_ge(xn1_done, HB * (half + 1))
                        hs = slice(half * HB, (half + 1) * HB)
                        pool.tensor_tensor(res[:, hs, :], res[:, hs, :], bias_sb[:].unsqueeze(1).to_broadcast([P, HB, P]),
                                           ALU.add).then_inc(bias_added, 1)
                    clear_rows(4)
                sum_self(p)
                rest_self(p)
                lo_self(p)

            for n in range(TAIL):
                if n + LEAD_PREP < NB:
                    clear_rows(n + LEAD_PREP)
                for g in range(NU):
                    u = n * NU + g
                    if NB * NU <= u < UNITS:
                        pool.wait_ge(exp_done, u + 1)
                        pool.affine_select(out=probs[:, u % PR, :], in_=probs[:, u % PR, :], compare_op=ALU.is_ge,
                                           fill=0.0, base=0, pattern=[[0, GH], [1, P]], channel_multiplier=-1)\
                            .then_inc(masked, 1)
                    if g == 0 and n >= 2:
                        inverse_std(slice(NB + n - 2, NB + n - 1), 2 + n - 1)
                    if g == 1:
                        if 1 <= n and n - 1 + LEAD_PREP < NB:
                            lo_self(n - 1 + LEAD_PREP)
                        if 0 <= n - 3 < NB:
                            m = n - 3
                            pool.wait_ge(midx_done, m + 1)
                            pool.tensor_tensor(parts_x[:, m % 2, 2], rest_x[:, m % 2], parts_x[:, m % 2, 1],
                                               ALU.subtract).then_inc(lox_done, 1)
                    if g == 3 and n + LEAD_PREP < NB:
                        sum_self(n + LEAD_PREP)
                        rest_self(n + LEAD_PREP)


_INS = ['x', 'ctx_1024', 'mask_BxS2_if1', 'L0_attn_w_qkv', 'L0_attn_w_proj', 'L0_attn_b_proj',
        'L0_xattn_Wq', 'L0_xattn_Wk', 'L0_xattn_Wv', 'L0_xattn_Wo',
        'L0_ffn_w_gate', 'L0_ffn_w1', 'L0_ffn_w3', 'L0_ffn_w2']


def _constants():
    import numpy as np
    c = np.zeros((P, NCONST), np.float32)
    c[:, C_ID:C_ID + P] = np.eye(P, dtype=np.float32)
    c[:, C_CAUSAL:C_CAUSAL + P] = np.where(np.tril(np.ones((P, P), bool)), 0.0, -BIG)
    inv = (1.0 / np.float32(10000.0) ** (np.arange(0, DH, 2, dtype=np.float32) / np.float32(DH))).astype(np.float32)
    ang = (np.arange(P, dtype=np.float32)[:, None] * inv[None, :]).astype(np.float32)
    f = np.arange(P)
    sign = np.where(f % DH < DH // 2, -1.0, 1.0).astype(np.float32)
    c[:, C_COS:C_COS + P] = np.cos(ang).T[f % (DH // 2)]
    c[:, C_SIN:C_SIN + P] = np.sin(ang).T[f % (DH // 2)] * sign[:, None]
    c[:, C_IOTA:C_IOTA + NE] = np.arange(NE)
    c[:, C_HALF:C_HALF + NE] = -0.5
    return c


def kernel(**inputs):
    import numpy as _np
    import concourse.bacc as _bacc
    from concourse import mybir as _mybir
    from concourse.bass_utils import run_bass_kernel_spmd as _run

    nc = _bacc.Bacc("TRN2", target_bir_lowering=False, num_devices=1)
    arrays, args = {}, []
    named = [(name, _np.ascontiguousarray(inputs[name])) for name in _INS] + [("const", _constants())]
    for name, a in named:
        arrays[f"in_{name}_dram"] = a
        args.append(nc.dram_tensor(f"in_{name}_dram", a.shape, _mybir.dt.from_np(a.dtype), kind="ExternalInput").ap())
    args.append(nc.dram_tensor("out_0_dram", (NB, P, P), _mybir.dt.float32, kind="ExternalOutput").ap())
    decoder_block(nc, *args)
    r = _run(nc, [arrays], core_ids=[0])
    return r.results[0]["out_0_dram"]
```

```python
from contextlib import ExitStack

import concourse.bass as bass
from concourse import mybir

ALU = mybir.AluOpType
ACT = mybir.ActivationFunctionType
AX = mybir.AxisListType
F32 = mybir.dt.float32
BF16 = mybir.dt.bfloat16
I32 = mybir.dt.int32
U32 = mybir.dt.uint32

P = 128
NB = 8
NH = 16
DH = P // NH
GH = 4
NU = NH // GH
NA = 2 * NB
UNITS = NA * NU
LEAD_UNITS = 7
LEAD_PREP = 5
FIRST = -LEAD_PREP
PR = 3
NE = 8
NHID = 256
NC = NHID // P
HB = NB // 2
SLOTS = 6
QK_ROWS = DH * SLOTS
ROWS = 96
ONES = 0x3F803F80
PAD_ROW = 48
SHIFT_ROW = 64
BIG = 1e30
EPS = 1e-5
SCALE = float(DH) ** -0.5
C_ID, C_CAUSAL, C_COS, C_SIN, C_IOTA, C_HALF = 0, P, 2 * P, 3 * P, 4 * P, 4 * P + NE
NCONST = 4 * P + 2 * NE


def decoder_block(nc, x, ctx_in, mask, w_qkv, w_proj, b_proj, wq, wk, wv, wo, w_gate, w1, w3, w2, const, out):
    with ExitStack() as stack:
        def sb(name, shape, dt):
            return stack.enter_context(nc.sbuf_tensor(name, shape, dt))

        def psum(name):
            return stack.enter_context(nc.psum_tensor(name, [P, 512], F32))

        def sem(name):
            return stack.enter_context(nc.semaphore(name))

        bank_a = [psum("bank_a0"), psum("bank_a1")]
        bank_b = [psum("bank_b0"), psum("bank_b1")]
        bank_r = [psum("bank_r0"), psum("bank_r1")]
        bank_m = psum("bank_m")
        bank_n = psum("bank_n")

        consts = sb("consts", [P, NCONST], F32)
        ident = consts[:, C_ID:C_ID + P]
        causal_f = consts[:, C_CAUSAL:C_CAUSAL + P]
        cos_t = consts[:, C_COS:C_COS + P]
        sin_t = consts[:, C_SIN:C_SIN + P]
        iota = consts[:, C_IOTA:C_IOTA + NE]
        minus_half = consts[:, C_HALF:C_HALF + NE]
        ident_h = sb("ident_h", [P, P], BF16)
        causal_h = sb("causal_h", [P, P], BF16)
        one_rows = sb("one_rows", [2, 4 * P], BF16)
        mask_i = sb("mask_i", [NB, P], I32)
        pad_rows = sb("pad_rows", [NB, P], BF16)

        wqkv_sb = sb("wqkv_sb", [P, 3 * P], F32)
        wswap = sb("wswap", [P, 2 * P], F32)
        wproj_sb = sb("wproj_sb", [P, P], F32)
        bias_sb = sb("bias_sb", [P, P], F32)
        wx_sb = sb("wx_sb", [P, 4, P], F32)
        wxT = sb("wxT", [P, 4, P], F32)
        gate_sb = sb("gate_sb", [P, NE], F32)
        w1_sb = sb("w1_sb", [P, NE, NHID], F32)
        w3_sb = sb("w3_sb", [P, NE, NHID], F32)
        w2_sb = sb("w2_sb", [P, NE, NC, P], F32)

        res = sb("res", [P, NB, P], F32)
        ctx_sb = sb("ctx_sb", [P, NB, P], F32)
        stats = sb("stats", [P, 3 * NB, 6], F32)
        mv = sb("mv", [P, 3 * NB, 2], F32)
        veps = sb("veps", [P, 3 * NB], F32)
        rstd = sb("rstd", [P, 3 * NB], F32)
        xn1 = sb("xn1", [P, NB, P], F32)
        xn = sb("xn", [P, 2, P], F32)
        x1T = sb("x1T", [P, NB, P], F32)
        x2T = sb("x2T", [P, 2, P], F32)
        x3T = x1T
        ctxT = sb("ctxT", [P, 2, P], F32)

        rot = sb("rot", [P, 2, 2, P], F32)
        rot_sw = sb("rot_sw", [P, 2, 2, P], F32)
        qk_f = sb("qk_f", [P, 2, 2, P], F32)
        rest = sb("rest", [P, 2, 2, P], F32)
        parts = sb("parts", [P, 2, 16, P], BF16)
        rest_x = sb("rest_x", [P, 2, 2, P], F32)
        parts_x = sb("parts_x", [P, 2, 16, P], BF16)
        q_room = sb("q_room", [P, NB, NH * P], BF16)
        q_rows = q_room[0:ROWS, :, :].rearrange("p b (h t) -> p b h t", h=NH)
        qx_rows = sb("qx_rows", [ROWS, NB, NH, P], BF16)
        k_rows = sb("k_rows", [ROWS, NB, NH, P], BF16)
        v_aug = sb("v_aug", [P, NB, NH, 32], F32)
        neg_max = sb("neg_max", [P, 2, NH], F32)
        neg_max_h = sb("neg_max_h", [P, 2, 2, NH], BF16)
        shift = sb("shift", [2 * NH, 2, P], BF16)
        nan_fix = sb("nan_fix", [P, 4, NH], F32)
        probs = sb("probs", [P, PR, GH * P], F32)
        r_sb = sb("r_sb", [P, GH * P], F32)
        rden = sb("rden", [P, NH], F32)
        attn_o = sb("attn_o", [P, P], F32)
        attn_oT = sb("attn_oT", [P, P], F32)

        logits = sb("logits", [P, NB, NE], F32)
        top = sb("top", [P, NB, 8], F32)
        top_i = sb("top_i", [P, NB, 8], U32)
        top_f = sb("top_f", [P, NB, 2], F32)
        gap = sb("gap", [P, NB], F32)
        e_gap = sb("e_gap", [P, NB], F32)
        gden = sb("gden", [P, NB], F32)
        prob1 = sb("prob1", [P, NB], F32)
        prob2 = sb("prob2", [P, NB], F32)
        pick1 = sb("pick1", [P, NB, NE], F32)
        pick2 = sb("pick2", [P, NB, NE], F32)
        gates = sb("gates", [P, NB, NE], F32)
        hid = q_room[:, 0:2, :].bitcast(F32).rearrange("p r (c t) -> p r c t", c=NC)
        silu_sb = q_room[:, 2, :].bitcast(F32).rearrange("p (c t) -> p c t", c=NC)

        scratch = nc.dram_tensor("scratch", (NA, 2, P, SLOTS, P), BF16, kind="Internal").ap()

        in_const, in_mask, in_wqkv, in_ctx = sem("in_const"), sem("in_mask"), sem("in_wqkv"), sem("in_ctx")
        in_wx, in_proj, in_gate, in_w13, in_w2 = sem("in_wx"), sem("in_proj"), sem("in_gate"), sem("in_w13"), sem("in_w2")
        in_x = [sem("in_x0"), sem("in_x1")]
        const_h = sem("const_h")
        q_zero = [sem(f"q_zero{b}") for b in range(NB)]
        k_zero, k_ones = sem("k_zero"), sem("k_ones")
        qx_zero, qx_ones = sem("qx_zero"), sem("qx_ones")
        v_zero, v_one = [sem("v_zero0"), sem("v_zero1")], sem("v_one")
        w_swapped, wxT_ready, wxT_taken = sem("w_swapped"), sem("wxT_ready"), sem("wxT_taken")
        stats_done, rstd_done, veps_done = sem("stats_done"), sem("rstd_done"), sem("veps_done")
        xn1_done, xn_done, bias_added = sem("xn1_done"), sem("xn_done"), sem("bias_added")
        x1T_ready, x1T_taken = sem("x1T_ready"), sem("x1T_taken")
        qkv_ready, rope_done, v_ready, v_taken = sem("qkv_ready"), sem("rope_done"), sem("v_ready"), sem("v_taken")
        sum_done, hi_done, rest_done, mid_done, lo_done, rep_done = (
            sem("sum_done"), sem("hi_done"), sem("rest_done"), sem("mid_done"), sem("lo_done"), sem("rep_done"))
        ctxT_ready, ctxT_taken = sem("ctxT_ready"), sem("ctxT_taken")
        qkvx_ready, hix_done, vx_taken = sem("qkvx_ready"), sem("hix_done"), sem("vx_taken")
        restx_done, midx_done, lox_done, repx_done = sem("restx_done"), sem("midx_done"), sem("lox_done"), sem("repx_done")
        written = [sem(f"written{n}") for n in range(NA)]
        stacked = [sem(f"stacked{n}") for n in range(NA)]
        shifted = [sem(f"shifted{n}") for n in range(NA)]
        sa_ready, max_done = sem("sa_ready"), sem("max_done")
        nmh_done, nmT_ready, nmT_taken, nan_done = sem("nmh_done"), sem("nmT_ready"), sem("nmT_taken"), sem("nan_done")
        sb_ready, exp_done, masked, pv_done = sem("sb_ready"), sem("exp_done"), sem("masked"), sem("pv_done")
        r_taken, rT_ready, norm_done = sem("r_taken"), sem("rT_ready"), sem("norm_done")
        oT_ready, oT_taken, proj_ready, res_done = sem("oT_ready"), sem("oT_taken"), sem("proj_ready"), sem("res_done")
        xT_ready, xT_taken = sem("xT_ready"), sem("xT_taken")
        gate_ready, logits_taken, gap_done, e_gap_done, gates_done = (
            sem("gate_ready"), sem("logits_taken"), sem("gap_done"), sem("e_gap_done"), sem("gates_done"))
        up_ready, silu_done, hid_done, down_ready, y_taken = (
            sem("up_ready"), sem("silu_done"), sem("hid_done"), sem("down_ready"), sem("y_taken"))
        out_done = sem("out_done")

        CHUNKS = 2 * NE
        items = []
        for k in range(CHUNKS + 1):
            if k < CHUNKS:
                items += [("up", k, c) for c in range(NC)]
            if k >= 1:
                items.append(("down", k - 1, 0))
        TAIL = NA + 2
        tail_steps = [(n, g) for n in range(NA, TAIL) for g in range(NU)]

        def items_behind(n, g):
            if (n, g) not in tail_steps:
                return []
            at = tail_steps.index((n, g))
            return items[at:at + 1] if at < len(tail_steps) - 1 else items[at:]

        block = stack.enter_context(nc.Block())

        @block.sync
        def _(sp):
            for half in range(2):
                sp.dma_start(res[:, half * HB:(half + 1) * HB, :],
                             x[half * HB:(half + 1) * HB].rearrange("b t c -> t b c")).then_inc(in_x[half], 16)
                if half == 0:
                    sp.dma_start(consts[:], const).then_inc(in_const, 16)
                    sp.dma_start(wqkv_sb[:], w_qkv).then_inc(in_wqkv, 16)
            sp.dma_start(mask_i[:], mask).then_inc(in_mask, 16)
            for i, w in enumerate((wq, wk, wv, wo)):
                sp.dma_start(wx_sb[:, i, :], w).then_inc(in_wx, 16)
            sp.dma_start(ctx_sb[:], ctx_in.rearrange("b t c -> t b c")).then_inc(in_ctx, 16)
            sp.dma_start(wproj_sb[:], w_proj).then_inc(in_proj, 16)
            sp.dma_start(bias_sb[:], b_proj.rearrange("(o c) -> o c", o=1).to_broadcast([P, P])).then_inc(in_proj, 16)
            sp.dma_start(gate_sb[:], w_gate).then_inc(in_gate, 16)

            def write_parts(n, tile):
                sp.dma_start(scratch[n].rearrange("a p s t -> p a (s t)"),
                             tile[:, 0:2 * SLOTS, :].rearrange("p (a s) t -> p a (s t)", a=2)).then_inc(written[n], 16)

            def read_rows(n, q_to):
                sp.wait_ge(written[n], 16)
                for t, to in enumerate((q_to, k_rows)):
                    sp.dma_start(to[0:QK_ROWS, n % NB, :, :],
                                 scratch[n, t].rearrange("(h d) s t -> (d s) h t", d=DH)).then_inc(stacked[n], 16)

            def put_shift(n):
                sp.wait_ge(nmT_taken, n + 1)
                sp.wait_ge(sa_ready, NU * (n + 1))
                rows = q_rows if n < NB else qx_rows
                sp.dma_start(rows[SHIFT_ROW:SHIFT_ROW + 2, n % NB, :, :], shift[:, n % 2, :])\
                    .then_inc(shifted[n], 16)

            sp.wait_ge(const_h, 1)
            sp.wait_ge(k_zero, NB)
            sp.dma_start(k_rows[SHIFT_ROW:SHIFT_ROW + 2, :, :, :],
                         one_rows[:].unsqueeze(1).to_broadcast([2, NB * NH // 4, 4 * P])).then_inc(k_ones, 16)
            sp.dma_start(k_rows[PAD_ROW:PAD_ROW + 1, :, :, :],
                         pad_rows[:].unsqueeze(1).to_broadcast([NB, NH, P])).then_inc(k_ones, 16)
            for n in range(FIRST, NA):
                p = n - 1 + LEAD_PREP
                if 0 <= p < NB:
                    sp.wait_ge(lo_done, p + 1)
                    sp.wait_ge(rep_done, p + 1)
                    write_parts(p, parts[:, p % 2])
                if n + 1 in range(NA):
                    put_shift(n + 1)
                if 0 <= p < NB:
                    sp.wait_ge(q_zero[p], 1)
                    read_rows(p, q_rows)
                if n == -1:
                    sp.dma_start(w1_sb[:], w1.rearrange("e d h -> d e h")).then_inc(in_w13, 16)
                    sp.dma_start(w3_sb[:], w3.rearrange("e d h -> d e h")).then_inc(in_w13, 16)
                    sp.dma_start(w2_sb[:], w2.rearrange("e (c p) d -> p e c d", p=P)).then_inc(in_w2, 16)
                b = n - 3
                if 0 <= b < NB:
                    if b == 0:
                        sp.wait_ge(qx_zero, NB)
                        sp.dma_start(qx_rows[PAD_ROW:PAD_ROW + 1, :, :, :],
                                     one_rows[0:1].unsqueeze(1).to_broadcast([1, NB * NH // 4, 4 * P]))\
                            .then_inc(qx_ones, 16)
                    sp.wait_ge(lox_done, b + 1)
                    sp.wait_ge(repx_done, b + 1)
                    write_parts(NB + b, parts_x[:, b % 2])
                    sp.wait_ge(sb_ready, NU * (b + 1))
                    read_rows(NB + b, qx_rows)
            for half in range(2):
                sp.wait_ge(y_taken, NE * (half + 1))
                sp.dma_start(out[half * HB:(half + 1) * HB].rearrange("b t c -> t b c"),
                             res[:, half * HB:(half + 1) * HB, :]).then_inc(out_done, 16)
            sp.wait_ge(out_done, 32)

        @block.tensor
        def _(pe):
            def transpose_x1(p, bank):
                pe.wait_ge(xn1_done, p + 1)
                pe.transpose(bank[:, 0:P], xn1[:, p, :], ident).then_inc(x1T_ready, 1)

            def project_qk(p, bank):
                pe.wait_ge(x1T_taken, p + 1)
                for i, w in enumerate((wqkv_sb[:, 0:P], wqkv_sb[:, P:2 * P], wswap[:, 0:P], wswap[:, P:2 * P])):
                    mm = pe.matmul(bank[:, i * P:(i + 1) * P], w, x1T[:, p, :], start=True, stop=True)
                mm.then_inc(qkv_ready, 1)

            def project_v(p, bank):
                pe.wait_ge(x1T_taken, p + 1)
                pe.matmul(bank[:, 3 * P:4 * P], x1T[:, p, :], wqkv_sb[:, 2 * P:3 * P],
                          start=True, stop=True).then_inc(v_ready, 1)

            def scores_a(u):
                n, g = divmod(u, NU)
                b = n % NB
                if g == 0:
                    pe.wait_ge(stacked[n], 32)
                if u == 0:
                    pe.wait_ge(k_ones, 32)
                if u == NB * NU:
                    pe.wait_ge(qx_ones, 16)
                q = q_rows if n < NB else qx_rows
                if u >= 2:
                    pe.wait_ge(max_done, u - 1)
                bank = bank_a[u % 2]
                for j in range(GH):
                    h = g * GH + j
                    mm = pe.matmul(bank[:, j * P:(j + 1) * P], q[:, b, h, :], k_rows[:, b, h, :],
                                   start=(n < NB or j == 0), stop=(n < NB), skip_group_check=True)
                if n >= NB:
                    mm = pe.matmul(bank[:, :], ident_h[:], causal_h[:].unsqueeze(1).to_broadcast([P, GH, P]),
                                   start=False, stop=True, skip_group_check=True)
                mm.then_inc(sa_ready, 1)

            def scores_b(u):
                n, g = divmod(u, NU)
                b = n % NB
                if g == 0:
                    pe.wait_ge(shifted[n], 16)
                if u >= 2:
                    pe.wait_ge(exp_done, u - 1)
                q = q_rows if n < NB else qx_rows
                for j in range(GH):
                    h = g * GH + j
                    mm = pe.matmul(bank_b[u % 2][:, j * P:(j + 1) * P], k_rows[:, b, h, :], q[:, b, h, :],
                                   start=True, stop=True)
                mm.then_inc(sb_ready, 1)

            def product_v(u):
                n, g = divmod(u, NU)
                if g == 0:
                    if n == 0:
                        pe.wait_ge(v_one, 2)
                    if n < NB:
                        pe.wait_ge(v_taken, n + 1)
                    else:
                        pe.wait_ge(vx_taken, n - NB + 1)
                    if n >= 2:
                        pe.wait_ge(r_taken, n - 1)
                if n < NB:
                    pe.wait_ge(exp_done, u + 1)
                else:
                    pe.wait_ge(masked, u - NB * NU + 1)
                for j in range(GH):
                    mm = pe.matmul(bank_r[n % 2][32 * j:32 * j + 32, g * P:(g + 1) * P],
                                   v_aug[:, n % NB, g * GH + j, :], probs[:, u % PR, j * P:(j + 1) * P],
                                   start=True, stop=True)
                mm.then_inc(pv_done, 1)

            def max_transpose(n):
                pe.wait_ge(nmh_done, n + 1)
                if n == 0:
                    pe.wait_ge(const_h, 1)
                pe.transpose(bank_n[0:2 * NH, 0:P // 2].bitcast(BF16),
                             neg_max_h[:, n % 2, :, :].rearrange("p a h -> p (a h)"), ident_h[:]).then_inc(nmT_ready, 1)

            def up(k, c):
                half, e = divmod(k, NE)
                if k == 0 and c == 0:
                    pe.wait_ge(in_w13, 32)
                    pe.wait_ge(max_done, UNITS)
                    pe.wait_ge(exp_done, UNITS)
                if k >= 1:
                    pe.wait_ge(silu_done, NC * (k - 1) + c + 1)
                    pe.wait_ge(hid_done, NC * (k - 1) + c + 1)
                if e == 0 and c == 0:
                    pe.wait_ge(xT_taken, NB + HB * (half + 1))
                rhs = x3T[:, half * HB:(half + 1) * HB, :].rearrange("p b t -> p (b t)")
                pe.matmul(bank_a[c][:, :], w1_sb[:, e, c * P:(c + 1) * P], rhs, start=True, stop=True)
                pe.matmul(bank_b[c][:, :], w3_sb[:, e, c * P:(c + 1) * P], rhs, start=True, stop=True)\
                    .then_inc(up_ready, 1)

            def down(k):
                if k == 0:
                    pe.wait_ge(in_w2, 16)
                    pe.wait_ge(r_taken, NA)
                if k >= 2:
                    pe.wait_ge(y_taken, k - 1)
                pe.wait_ge(hid_done, NC * (k + 1))
                for bb in range(HB):
                    for c in range(NC):
                        mm = pe.matmul(bank_r[k % 2][:, bb * P:(bb + 1) * P], hid[:, k % 2, c, bb * P:(bb + 1) * P],
                                       w2_sb[:, k % NE, c, :], start=(c == 0), stop=(c == NC - 1))
                mm.then_inc(down_ready, 1)

            pe.wait_ge(in_const, 16)
            for n in range(FIRST, TAIL):
                for g in range(NU):
                    u = n * NU + g
                    if 0 <= u + LEAD_UNITS < UNITS:
                        scores_a(u + LEAD_UNITS)
                    if 0 <= u < UNITS:
                        scores_b(u)
                    if 1 <= u <= UNITS:
                        product_v(u - 1)
                    if g == 0:
                        if n + LEAD_PREP < NB or 0 <= n - 2 < NB:
                            if n == 0:
                                pe.wait_ge(wxT_taken, 1)
                            elif n >= 2:
                                pe.wait_ge(res_done, n - 1)
                        if n + LEAD_PREP < NB:
                            transpose_x1(n + LEAD_PREP, bank_m)
                        if 0 <= n - 2 < NB:
                            if n == 2:
                                pe.wait_ge(in_ctx, 16)
                            if n >= 4:
                                pe.wait_ge(qkvx_ready, n - 3)
                            pe.transpose(bank_m[:, P:2 * P], ctx_sb[:, n - 2, :], ident).then_inc(ctxT_ready, 1)
                    if g == 1:
                        if 0 <= n + 1 < NA:
                            if 0 <= n - 1 + LEAD_PREP < NB:
                                pe.wait_ge(v_taken, n + LEAD_PREP)
                            if 0 <= n - 3 < NB:
                                pe.wait_ge(vx_taken, n - 2)
                                pe.wait_ge(restx_done, n - 2)
                            if n - 1 >= NB + 2:
                                pe.wait_ge(logits_taken, n - NB - 2)
                            max_transpose(n + 1)
                        if 1 <= n <= NA:
                            if n + LEAD_PREP < NB:
                                pe.wait_ge(x1T_taken, n + LEAD_PREP + 1)
                            if 0 <= n - 2 < NB:
                                pe.wait_ge(ctxT_taken, n - 1)
                            elif n >= 2:
                                pe.wait_ge(res_done, n - 1)
                            pe.wait_ge(r_taken, n)
                            for i in range(GH):
                                mm = pe.transpose(bank_m[:, i * P:(i + 1) * P], r_sb[:, i * P:(i + 1) * P], ident)
                            mm.then_inc(rT_ready, 1)
                    if g == 2:
                        if n + LEAD_PREP < NB:
                            if n + 1 >= 0:
                                pe.wait_ge(nmT_taken, n + 2)
                            elif n > FIRST:
                                pe.wait_ge(v_taken, n + LEAD_PREP)
                            if n == FIRST:
                                pe.wait_ge(in_wqkv, 16)
                                pe.wait_ge(w_swapped, 1)
                            project_qk(n + LEAD_PREP, bank_n)
                        if 1 <= n <= NA:
                            pe.wait_ge(norm_done, n)
                            pe.transpose(bank_m[:, 0:P], attn_o[:], ident).then_inc(oT_ready, 1)
                        if n >= 2:
                            if n > NA:
                                pe.wait_ge(res_done, n - 1)
                            pe.wait_ge(xn_done, n - 1)
                            pe.transpose(bank_m[:, P:2 * P], xn[:, n % 2, :], ident).then_inc(xT_ready, 1)
                    if g == 3:
                        if n + LEAD_PREP < NB:
                            pe.wait_ge(rope_done, n + LEAD_PREP + 1)
                            project_v(n + LEAD_PREP, bank_n)
                            if n == -1:
                                pe.wait_ge(in_wx, 64)
                                for i in range(4):
                                    mm = pe.transpose(bank_m[:, i * P:(i + 1) * P], wx_sb[:, i, :], ident)
                                mm.then_inc(wxT_ready, 1)
                        elif n + 1 < NA:
                            pe.wait_ge(nmT_taken, n + 2)
                        if 0 <= n - 2 < NB:
                            m = n - 2
                            pe.wait_ge(xT_taken, m + 1)
                            pe.wait_ge(ctxT_taken, m + 1)
                            pe.matmul(bank_n[:, 0:P], wxT[:, 0, :], x2T[:, m % 2, :], start=True, stop=True)
                            pe.matmul(bank_n[:, P:2 * P], wxT[:, 1, :], ctxT[:, m % 2, :], start=True, stop=True)
                            pe.matmul(bank_n[:, 2 * P:3 * P], ctxT[:, m % 2, :], wxT[:, 2, :], start=True, stop=True)\
                                .then_inc(qkvx_ready, 1)
                        if n - 2 >= NB:
                            m = n - 2 - NB
                            if n == NB + 2:
                                pe.wait_ge(in_gate, 16)
                            if m >= 1:
                                pe.wait_ge(logits_taken, m)
                            pe.wait_ge(xT_taken, n - 1)
                            pe.matmul(bank_n[:, 0:NE], x3T[:, m, :], gate_sb[:], start=True, stop=True)\
                                .then_inc(gate_ready, 1)
                        if 1 <= n <= NA:
                            pe.wait_ge(oT_taken, n)
                            if n >= 2:
                                pe.wait_ge(xT_taken, n - 1)
                            if n == 1:
                                pe.wait_ge(in_proj, 32)
                            pe.matmul(bank_m[:, 0:P], attn_oT[:], wproj_sb[:] if n <= NB else wxT[:, 3, :],
                                      start=True, stop=True).then_inc(proj_ready, 1)
                    for kind, k, c in items_behind(n, g):
                        if kind == "up":
                            up(k, c)
                        else:
                            down(k)

        @block.scalar
        def _(act):
            def clear(rows, b, done):
                act.memzero(rows[:, b].rearrange("p h t -> p (h t)")).then_inc(done, 1)

            def copy_x1T(p, bank):
                act.wait_ge(x1T_ready, p + 1)
                act.activation(x1T[:, p, :], bank[:, 0:P], ACT.Copy).then_inc(x1T_taken, 1)

            def copy_v(p, bank):
                act.wait_ge(v_ready, p + 1)
                act.activation(v_aug[:, p, :, 0:DH], bank[:, 3 * P:4 * P].rearrange("p (h d) -> p h d", h=NH), ACT.Copy)\
                    .then_inc(v_taken, 1)

            def hi_self(p):
                act.wait_ge(sum_done, p + 1)
                if p >= 2:
                    act.wait_ge(written[p - 2], 16)
                act.activation(parts[:, p % 2, 0:9:8, :], qk_f[:, p % 2], ACT.Copy).then_inc(hi_done, 1)

            def mid_self(p):
                act.wait_ge(rest_done, p + 1)
                act.activation(parts[:, p % 2, 3:8:4, :], rest[:, p % 2], ACT.Copy).then_inc(mid_done, 1)

            def hi_cross(m):
                act.wait_ge(qkvx_ready, m + 1)
                act.wait_ge(pv_done, NU * (m + 1))
                act.activation(v_aug[:, m, :, 0:DH], bank_n[:, 2 * P:3 * P].rearrange("p (h d) -> p h d", h=NH), ACT.Copy)\
                    .then_inc(vx_taken, 1)
                if m >= 2:
                    act.wait_ge(written[NB + m - 2], 16)
                act.activation(parts_x[:, m % 2, 0:9:8, :], bank_n[:, 0:2 * P].rearrange("p (a t) -> p a t", a=2), ACT.Copy)\
                    .then_inc(hix_done, 1)

            def mid_cross(m):
                act.wait_ge(restx_done, m + 1)
                act.activation(parts_x[:, m % 2, 3:8:4, :], rest_x[:, m % 2], ACT.Copy).then_inc(midx_done, 1)

            def silu(k, c):
                act.wait_ge(up_ready, NC * k + c + 1)
                if k >= 1:
                    act.wait_ge(hid_done, NC * (k - 1) + c + 1)
                elif c == 0:
                    act.wait_ge(sb_ready, NB * NU)
                act.activation(silu_sb[:, c, :], bank_a[c][:, :], ACT.Silu).then_inc(silu_done, 1)

            for b in range(2, 5):
                clear(k_rows, b, k_zero)
            act.memzero(v_aug[:, 0:HB].rearrange("p b h c -> p (b h c)")).then_inc(v_zero[0], 1)
            for b in range(1, 3):
                clear(q_rows, b, q_zero[b])
            act.wait_ge(v_zero[0], 1)

            for n in range(FIRST, TAIL):
                for g in range(NU):
                    u = n * NU + g
                    if 0 <= u < UNITS:
                        act.wait_ge(sb_ready, u + 1)
                        if u >= PR:
                            act.wait_ge(pv_done, u - PR + 1)
                        act.activation(probs[:, u % PR, :], bank_b[u % 2][:, :], ACT.Exp, scale=SCALE)\
                            .then_inc(exp_done, 1)
                    if g == 0:
                        if 1 <= n <= NA:
                            act.wait_ge(pv_done, NU * n)
                            if n >= 2:
                                act.wait_ge(rT_ready, n - 1)
                            act.activation(r_sb[:], bank_r[(n - 1) % 2][:, :], ACT.Copy).then_inc(r_taken, 1)
                        if 0 <= n - 2 < NB:
                            act.wait_ge(ctxT_ready, n - 1)
                        if n + LEAD_PREP < NB:
                            copy_x1T(n + LEAD_PREP, bank_m)
                        if 0 <= n - 2 < NB:
                            act.activation(ctxT[:, n % 2, :], bank_m[:, P:2 * P], ACT.Copy).then_inc(ctxT_taken, 1)
                    if g == 1:
                        if 0 <= n - 1 + LEAD_PREP < NB:
                            mid_self(n - 1 + LEAD_PREP)
                        if 0 <= n - 3 < NB:
                            mid_cross(n - 3)
                    if g == 2:
                        if n >= 2:
                            act.wait_ge(xT_ready, n - 1)
                        if 1 <= n <= NA:
                            act.wait_ge(oT_ready, n)
                            if n >= 2:
                                act.wait_ge(proj_ready, n - 1)
                            act.activation(attn_oT[:], bank_m[:, 0:P], ACT.Copy).then_inc(oT_taken, 1)
                        if n >= 2:
                            m = n - 2
                            if 2 <= m < NB:
                                act.wait_ge(qkvx_ready, m - 1)
                            act.activation(x2T[:, m % 2, :] if m < NB else x3T[:, m - NB, :], bank_m[:, P:2 * P],
                                           ACT.Copy).then_inc(xT_taken, 1)
                    if g == 3:
                        if n + LEAD_PREP < NB:
                            hi_self(n + LEAD_PREP)
                            if n >= 2:
                                act.wait_ge(qkvx_ready, n - 1)
                            if n + LEAD_PREP == HB:
                                act.wait_ge(v_zero[1], 1)
                            copy_v(n + LEAD_PREP, bank_n)
                        if n == -1:
                            act.wait_ge(wxT_ready, 1)
                            act.activation(wxT[:], bank_m[:, :].rearrange("p (a t) -> p a t", a=4), ACT.Copy)\
                                .then_inc(wxT_taken, 1)
                        if 0 <= n - 2 < NB:
                            hi_cross(n - 2)
                        if n in (NB + 2 + HB - 1, TAIL - 1):
                            half = 0 if n < TAIL - 1 else 1
                            hs = slice(half * HB, (half + 1) * HB)
                            act.wait_ge(gap_done, half + 1)
                            act.activation(e_gap[:, hs], gap[:, hs], ACT.Exp).then_inc(e_gap_done, 1)
                    for kind, k, c in items_behind(n, g):
                        if kind == "up":
                            silu(k, c)

        @block.vector
        def _(dve):
            steps = [0]
            dve_step = sem("dve_step")

            def then(ins):
                steps[0] += 1
                ins.then_inc(dve_step, 1)
                dve.wait_ge(dve_step, steps[0])

            def repeat(tile):
                by8 = tile.rearrange("p (a s) t -> p a s t", a=2)
                dve.tensor_copy(by8[:, :, 1:3, :], by8[:, :, 0:1, :].to_broadcast([P, 2, 2, P]))
                return dve.tensor_copy(tile[:, 5:12:6, :], tile[:, 3:8:4, :])

            def repeat_self(p):
                dve.wait_ge(mid_done, p + 1)
                repeat(parts[:, p % 2]).then_inc(rep_done, 1)

            def norm_stats(src, slot):
                then(dve.bn_stats(stats[:, slot, :], src))
                dve.bn_aggr(mv[:, slot, :], stats[:, slot, :]).then_inc(stats_done, 1)

            def normalise(dst, src, slot, done):
                dve.tensor_scalar(dst, src, mv[:, slot, 0:1], rstd[:, slot:slot + 1], ALU.subtract, ALU.mult)\
                    .then_inc(done, 1)

            def maximum(u):
                n, g = divmod(u, NU)
                dve.wait_ge(sa_ready, u + 1)
                if g == 0 and n >= 2:
                    dve.wait_ge(nmh_done, n - 1)
                    if n >= NB + 2:
                        dve.wait_ge(nan_done, n - 1 - NB)
                dve.tensor_reduce(neg_max[:, n % 2, g * GH:(g + 1) * GH],
                                  bank_a[u % 2][:, :].rearrange("p (h k) -> p h k", h=GH), AX.X, ALU.max, negate=True)\
                    .then_inc(max_done, 1)

            def split_max(n):
                dve.wait_ge(max_done, NU * (n + 1))
                if n >= 2:
                    dve.wait_ge(nmT_ready, n - 1)
                then(dve.tensor_copy(neg_max_h[:, n % 2, 0, :], neg_max[:, n % 2, :]))
                dve.tensor_tensor(neg_max_h[:, n % 2, 1, :], neg_max[:, n % 2, :], neg_max_h[:, n % 2, 0, :],
                                  ALU.subtract).then_inc(nmh_done, 1)
                if n >= NB:
                    if n >= NB + 4:
                        dve.wait_ge(norm_done, n - 3)
                    dve.tensor_scalar(nan_fix[:, n % 4, :], neg_max[:, n % 2, :], 1e10, 0.0, ALU.mult, ALU.mult)\
                        .then_inc(nan_done, 1)

            def take_max(n):
                dve.wait_ge(nmT_ready, n + 1)
                if n >= 2:
                    dve.wait_ge(shifted[n - 2], 16)
                dve.tensor_copy(shift[:, n % 2, :], bank_n[0:2 * NH, 0:P // 2].bitcast(BF16)).then_inc(nmT_taken, 1)

            def rope(p, bank):
                dve.wait_ge(qkv_ready, p + 1)
                if p >= 2:
                    dve.wait_ge(sum_done, p - 1)
                v = bank[:, :].rearrange("p (a t) -> p a t", a=4)
                dve.tensor_tensor(rot[:, p % 2], v[:, 0:2, :], cos_t.unsqueeze(1).to_broadcast([P, 2, P]), ALU.mult)
                dve.tensor_tensor(rot_sw[:, p % 2], v[:, 2:4, :], sin_t.unsqueeze(1).to_broadcast([P, 2, P]), ALU.mult)\
                    .then_inc(rope_done, 1)

            def divide(n):
                dve.wait_ge(rT_ready, n + 1)
                v = bank_m[:, :].rearrange("p (h c) -> p h c", c=32)
                then(dve.reciprocal(rden[:], v[:, :, DH]))
                if n >= NB:
                    dve.wait_ge(nan_done, n - NB + 1)
                    then(dve.tensor_tensor(rden[:], rden[:], nan_fix[:, n % 4, :], ALU.add))
                if n >= 1:
                    dve.wait_ge(oT_ready, n)
                dve.tensor_tensor(attn_o[:].rearrange("p (h d) -> p h d", h=NH), v[:, :, 0:DH],
                                  rden[:].unsqueeze(2).to_broadcast([P, NH, DH]), ALU.mult).then_inc(norm_done, 1)

            def add_residual(n):
                b = n % NB
                dve.wait_ge(proj_ready, n + 1)
                if n % HB == 0 and n < NB:
                    dve.wait_ge(bias_added, n // HB + 1)
                if n >= NB:
                    dve.wait_ge(res_done, n - NB + 1)
                dve.tensor_tensor(res[:, b, :], bank_m[:, 0:P], res[:, b, :], ALU.add).then_inc(res_done, 1)
                dve.wait_ge(res_done, n + 1)
                norm_stats(res[:, b, :], NB + n)

            def gating(half):
                hs = slice(half * HB, (half + 1) * HB)
                wide = [P, HB, NE]
                for b in range(half * HB, (half + 1) * HB):
                    then(dve.max(out=top[:, b, :], in_=logits[:, b, :]))
                    then(dve.max_index(out=top_i[:, b, :], in_max=top[:, b, :], in_values=logits[:, b, :]))
                dve.tensor_tensor(gap[:, hs], top[:, hs, 1], top[:, hs, 0], ALU.subtract).then_inc(gap_done, 1)
                then(dve.tensor_copy(top_f[:, hs, :], top_i[:, hs, 0:2]))
                for i, pick in enumerate((pick1, pick2)):
                    then(dve.tensor_tensor(pick[:, hs, :], iota.unsqueeze(1).to_broadcast(wide),
                                           top_f[:, hs, i].unsqueeze(2).to_broadcast(wide), ALU.is_equal))
                dve.wait_ge(e_gap_done, half + 1)
                then(dve.tensor_scalar(gden[:, hs], e_gap[:, hs], 1.0, None, ALU.add))
                then(dve.reciprocal(prob1[:, hs], gden[:, hs]))
                then(dve.tensor_tensor(prob2[:, hs], e_gap[:, hs], prob1[:, hs], ALU.mult))
                then(dve.tensor_tensor(pick1[:, hs, :], pick1[:, hs, :], prob1[:, hs].unsqueeze(2).to_broadcast(wide), ALU.mult))
                then(dve.tensor_tensor(pick2[:, hs, :], pick2[:, hs, :], prob2[:, hs].unsqueeze(2).to_broadcast(wide), ALU.mult))
                dve.tensor_tensor(gates[:, hs, :], pick1[:, hs, :], pick2[:, hs, :], ALU.add).then_inc(gates_done, 1)

            def hidden(k, c):
                dve.wait_ge(silu_done, NC * k + c + 1)
                if k == 0 and c == 0:
                    dve.wait_ge(sb_ready, NB * NU)
                if k >= 2 and c == 0:
                    dve.wait_ge(down_ready, k - 1)
                dve.tensor_tensor(hid[:, k % 2, c, :], bank_b[c][:, :], silu_sb[:, c, :], ALU.mult).then_inc(hid_done, 1)

            def add_expert(k):
                half, e = divmod(k, NE)
                dve.wait_ge(down_ready, k + 1)
                if e == 0:
                    dve.wait_ge(gates_done, half + 1)
                    dve.wait_ge(res_done, NB + HB * (half + 1))
                if k >= 1:
                    dve.wait_ge(y_taken, k)
                for bb in range(HB):
                    b = half * HB + bb
                    ins = dve.scalar_tensor_tensor(out=res[:, b, :], in0=bank_r[k % 2][:, bb * P:(bb + 1) * P],
                                                   scalar=gates[:, b, e:e + 1], in1=res[:, b, :],
                                                   op0=ALU.mult, op1=ALU.add)
                ins.then_inc(y_taken, 1)

            dve.memset(one_rows[:].bitcast(U32), ONES)
            for b in range(2):
                dve.memset(k_rows[:, b].bitcast(U32), 0).then_inc(k_zero, 1)
            dve.memset(q_rows[:, 0].bitcast(U32), 0).then_inc(q_zero[0], 1)
            dve.wait_ge(in_x[0], 16)
            for b in range(HB):
                norm_stats(res[:, b, :], b)
            dve.wait_ge(in_const, 16)
            dve.wait_ge(in_wqkv, 16)
            src = wqkv_sb[:, 0:2 * P].rearrange("p (h s j) -> p h s j", s=2, j=DH // 2)
            dst = wswap[:].rearrange("p (h s j) -> p h s j", s=2, j=DH // 2)
            dve.tensor_copy(dst[:, :, 0, :], src[:, :, 1, :])
            dve.tensor_copy(dst[:, :, 1, :], src[:, :, 0, :]).then_inc(w_swapped, 1)
            dve.tensor_copy(ident_h[:], ident)
            dve.tensor_copy(causal_h[:], causal_f)
            dve.wait_ge(in_mask, 16)
            dve.tensor_scalar(pad_rows[:], mask_i[:], 0.0, -BIG, ALU.is_equal, ALU.mult).then_inc(const_h, 1)
            dve.wait_ge(rstd_done, 1)
            for b in range(HB):
                normalise(xn1[:, b, :], res[:, b, :], b, xn1_done)
            dve.wait_ge(v_zero[0], 1)
            dve.memset(v_aug[:, 0:HB, :, DH], 1.0).then_inc(v_one, 1)

            for n in range(FIRST, TAIL):
                for g in range(NU):
                    u = n * NU + g
                    if 0 <= u + LEAD_UNITS < UNITS:
                        maximum(u + LEAD_UNITS)
                    if g == 0:
                        if 0 <= n + 1 < NA:
                            split_max(n + 1)
                        if n >= 2:
                            add_residual(n - 2)
                    if g == 1:
                        if 0 <= n + 1 < NA:
                            take_max(n + 1)
                        if 1 <= n <= NA:
                            divide(n - 1)
                        if n >= 2:
                            dve.wait_ge(rstd_done, 2 + n - 1)
                            if n >= 4:
                                dve.wait_ge(xT_ready, n - 3)
                            normalise(xn[:, n % 2, :], res[:, (n - 2) % NB, :], NB + n - 2, xn_done)
                    if g == 2:
                        if 0 <= n - 1 + LEAD_PREP < NB:
                            repeat_self(n - 1 + LEAD_PREP)
                        if n + LEAD_PREP < NB:
                            rope(n + LEAD_PREP, bank_n)
                        if 0 <= n - 3 < NB:
                            dve.wait_ge(midx_done, n - 2)
                            repeat(parts_x[:, (n - 3) % 2]).then_inc(repx_done, 1)
                    if g == 3:
                        if n == FIRST:
                            dve.wait_ge(in_x[1], 16)
                            for b in range(HB, NB):
                                norm_stats(res[:, b, :], b)
                        if n == FIRST + 1:
                            dve.wait_ge(rstd_done, 2)
                            for b in range(HB, NB):
                                normalise(xn1[:, b, :], res[:, b, :], b, xn1_done)
                            dve.wait_ge(v_zero[1], 1)
                            dve.memset(v_aug[:, HB:NB, :, DH], 1.0).then_inc(v_one, 1)
                        if 0 <= n - 2 < NB:
                            m = n - 2
                            dve.wait_ge(hix_done, m + 1)
                            if m >= 2:
                                dve.wait_ge(lox_done, m - 1)
                            dve.tensor_tensor(rest_x[:, m % 2], bank_n[:, 0:2 * P].rearrange("p (a t) -> p a t", a=2),
                                              parts_x[:, m % 2, 0:9:8, :], ALU.subtract).then_inc(restx_done, 1)
                        if n - 2 >= NB:
                            m = n - 2 - NB
                            dve.wait_ge(gate_ready, m + 1)
                            dve.tensor_copy(logits[:, m, :], bank_n[:, 0:NE]).then_inc(logits_taken, 1)
                            if m % HB == HB - 1:
                                dve.wait_ge(logits_taken, m + 1)
                                gating(m // HB)
                    for kind, k, c in items_behind(n, g):
                        if kind == "up":
                            hidden(k, c)
                        else:
                            add_expert(k)

        @block.gpsimd
        def _(pool):
            def clear(rows, b, done):
                pool.memset(rows[:, b].bitcast(U32), 0).then_inc(done, 1)

            def inverse_std(slots, count):
                pool.wait_ge(stats_done, slots.stop)
                pool.tensor_scalar(veps[:, slots], mv[:, slots, 1], EPS, 1.0, ALU.add, ALU.mult).then_inc(veps_done, 1)
                pool.wait_ge(veps_done, count)
                pool.tensor_tensor(rstd[:, slots], veps[:, slots], minus_half[:, 0:slots.stop - slots.start], ALU.pow)\
                    .then_inc(rstd_done, 1)

            def sum_self(p):
                pool.wait_ge(rope_done, p + 1)
                if p >= 2:
                    pool.wait_ge(hi_done, p - 1)
                    pool.wait_ge(rest_done, p - 1)
                pool.tensor_tensor(qk_f[:, p % 2], rot[:, p % 2], rot_sw[:, p % 2], ALU.add).then_inc(sum_done, 1)

            def rest_self(p):
                pool.wait_ge(sum_done, p + 1)
                pool.wait_ge(hi_done, p + 1)
                if p >= 2:
                    pool.wait_ge(lo_done, p - 1)
                pool.tensor_tensor(rest[:, p % 2], qk_f[:, p % 2], parts[:, p % 2, 0:9:8, :],
                                   ALU.subtract).then_inc(rest_done, 1)

            def lo_self(p):
                pool.wait_ge(rest_done, p + 1)
                pool.wait_ge(mid_done, p + 1)
                pool.tensor_tensor(parts[:, p % 2, 4:7:2, :], rest[:, p % 2], parts[:, p % 2, 3:8:4, :], ALU.subtract).then_inc(lo_done, 1)

            for b in range(5, NB):
                clear(k_rows, b, k_zero)
            pool.wait_ge(in_const, 16)
            inverse_std(slice(0, HB), 1)
            pool.memset(v_aug[:, HB:NB], 0.0).then_inc(v_zero[1], 1)

            for n in range(FIRST, TAIL):
                if 3 <= n + LEAD_PREP < NB:
                    clear(q_rows, n + LEAD_PREP, q_zero[n + LEAD_PREP])
                if n >= 0:
                    for b in range(3 * n, min(3 * n + 3, NB)):
                        clear(qx_rows, b, qx_zero)
                if n == FIRST + 1:
                    inverse_std(slice(HB, NB), 2)
                if n == FIRST + 3:
                    pool.wait_ge(in_proj, 32)
                    pool.wait_ge(xn1_done, NB)
                    for half in range(2):
                        hs = slice(half * HB, (half + 1) * HB)
                        pool.tensor_tensor(res[:, hs, :], res[:, hs, :], bias_sb[:].unsqueeze(1).to_broadcast([P, HB, P]),
                                           ALU.add).then_inc(bias_added, 1)
                for g in range(NU):
                    u = n * NU + g
                    if NB * NU <= u < UNITS:
                        pool.wait_ge(exp_done, u + 1)
                        pool.affine_select(out=probs[:, u % PR, :], in_=probs[:, u % PR, :], compare_op=ALU.is_ge,
                                           fill=0.0, base=0, pattern=[[0, GH], [1, P]], channel_multiplier=-1)\
                            .then_inc(masked, 1)
                    if g == 0 and n >= 2:
                        inverse_std(slice(NB + n - 2, NB + n - 1), 2 + n - 1)
                    if g == 1:
                        if 0 <= n - 1 + LEAD_PREP < NB:
                            lo_self(n - 1 + LEAD_PREP)
                        if 0 <= n - 3 < NB:
                            m = n - 3
                            pool.wait_ge(midx_done, m + 1)
                            pool.tensor_tensor(parts_x[:, m % 2, 4:7:2, :], rest_x[:, m % 2], parts_x[:, m % 2, 3:8:4, :],
                                               ALU.subtract).then_inc(lox_done, 1)
                    if g == 3 and n + LEAD_PREP < NB:
                        sum_self(n + LEAD_PREP)
                        rest_self(n + LEAD_PREP)


_INS = ['x', 'ctx_1024', 'mask_BxS2_if1', 'L0_attn_w_qkv', 'L0_attn_w_proj', 'L0_attn_b_proj',
        'L0_xattn_Wq', 'L0_xattn_Wk', 'L0_xattn_Wv', 'L0_xattn_Wo',
        'L0_ffn_w_gate', 'L0_ffn_w1', 'L0_ffn_w3', 'L0_ffn_w2']


def _constants():
    import numpy as np
    c = np.zeros((P, NCONST), np.float32)
    c[:, C_ID:C_ID + P] = np.eye(P, dtype=np.float32)
    c[:, C_CAUSAL:C_CAUSAL + P] = np.where(np.tril(np.ones((P, P), bool)), 0.0, -BIG)
    inv = (1.0 / np.float32(10000.0) ** (np.arange(0, DH, 2, dtype=np.float32) / np.float32(DH))).astype(np.float32)
    ang = (np.arange(P, dtype=np.float32)[:, None] * inv[None, :]).astype(np.float32)
    f = np.arange(P)
    sign = np.where(f % DH < DH // 2, -1.0, 1.0).astype(np.float32)
    c[:, C_COS:C_COS + P] = np.cos(ang).T[f % (DH // 2)]
    c[:, C_SIN:C_SIN + P] = np.sin(ang).T[f % (DH // 2)] * sign[:, None]
    c[:, C_IOTA:C_IOTA + NE] = np.arange(NE)
    c[:, C_HALF:C_HALF + NE] = -0.5
    return c


def kernel(**inputs):
    import numpy as _np
    import concourse.bacc as _bacc
    from concourse import mybir as _mybir
    from concourse.bass_utils import run_bass_kernel_spmd as _run

    nc = _bacc.Bacc("TRN2", target_bir_lowering=False, num_devices=1)
    arrays, args = {}, []
    named = [(name, _np.ascontiguousarray(inputs[name])) for name in _INS] + [("const", _constants())]
    for name, a in named:
        arrays[f"in_{name}_dram"] = a
        args.append(nc.dram_tensor(f"in_{name}_dram", a.shape, _mybir.dt.from_np(a.dtype), kind="ExternalInput").ap())
    args.append(nc.dram_tensor("out_0_dram", (NB, P, P), _mybir.dt.float32, kind="ExternalOutput").ap())
    decoder_block(nc, *args)
    r = _run(nc, [arrays], core_ids=[0])
    return r.results[0]["out_0_dram"]
```

```python
from contextlib import ExitStack

import concourse.bass as bass
from concourse import mybir

ALU = mybir.AluOpType
ACT = mybir.ActivationFunctionType
AX = mybir.AxisListType
F32 = mybir.dt.float32
F32R = mybir.dt.float32r
BF16 = mybir.dt.bfloat16
I32 = mybir.dt.int32
U32 = mybir.dt.uint32

P = 128
NB = 8
NH = 16
DH = P // NH
GH = 4
NU = NH // GH
NA = 2 * NB
UNITS = NA * NU
LEAD_UNITS = 9
LEAD_PREP = 6
START = 6
FIRST = START - LEAD_PREP
LAG = 2
FIRST_WEIGHTS = 12
PR = 3
NE = 8
NHID = 256
NC = NHID // P
HB = NB // 2
SLOTS = 6
QK_ROWS = DH * SLOTS
ROWS = 96
ONES = 0x3F803F80
PAD_ROW = 48
SHIFT_ROW = 64
BIG = 1e30
EPS = 1e-5
SCALE = float(DH) ** -0.5
C_ID, C_CAUSAL, C_COS, C_SIN, C_IOTA, C_HALF = 0, P, 2 * P, 3 * P, 4 * P, 4 * P + NE
NCONST = 4 * P + 2 * NE


def decoder_block(nc, x, ctx_in, mask, w_qkv, w_proj, b_proj, wq, wk, wv, wo, w_gate, w1, w3, w2, const, out):
    with ExitStack() as stack:
        def sb(name, shape, dt):
            return stack.enter_context(nc.sbuf_tensor(name, shape, dt))

        def psum(name):
            return stack.enter_context(nc.psum_tensor(name, [P, 512], F32))

        def sem(name):
            return stack.enter_context(nc.semaphore(name))

        bank_a = [psum("bank_a0"), psum("bank_a1")]
        bank_b = [psum("bank_b0"), psum("bank_b1")]
        bank_r = [psum("bank_r0"), psum("bank_r1")]
        bank_m = psum("bank_m")
        bank_n = psum("bank_n")

        consts = sb("consts", [P, NCONST], F32)
        ident = consts[:, C_ID:C_ID + P]
        causal_f = consts[:, C_CAUSAL:C_CAUSAL + P]
        cos_t = consts[:, C_COS:C_COS + P]
        sin_t = consts[:, C_SIN:C_SIN + P]
        iota = consts[:, C_IOTA:C_IOTA + NE]
        minus_half = consts[:, C_HALF:C_HALF + NE]
        ident_h = sb("ident_h", [P, P], BF16)
        causal_h = sb("causal_h", [P, P], BF16)
        one_rows = sb("one_rows", [2, 4 * P], BF16)
        mask_i = sb("mask_i", [NB, P], I32)
        pad_rows = sb("pad_rows", [NB, P], BF16)

        wqkv_sb = sb("wqkv_sb", [P, 3 * P], F32)
        wswap = sb("wswap", [P, 2 * P], F32)
        wproj_sb = sb("wproj_sb", [P, P], F32)
        bias_sb = sb("bias_sb", [P, P], F32)
        wx_sb = sb("wx_sb", [P, 4, P], F32)
        wxT = sb("wxT", [P, 4, P], F32)
        gate_sb = sb("gate_sb", [P, NE], F32)
        w_hi = sb("w_hi", [P, 2, 2, NHID], F32R)
        w_lo = sb("w_lo", [P, 2, 2, NHID], F32R)
        w2_sb = sb("w2_sb", [P, NE, NC, P], F32)

        res = sb("res", [P, NB, P], F32)
        ctx_sb = sb("ctx_sb", [P, NB, P], F32)
        stats = sb("stats", [P, 3 * NB, 6], F32)
        mv = sb("mv", [P, 3 * NB, 2], F32)
        veps = sb("veps", [P, 3 * NB], F32)
        rstd = sb("rstd", [P, 3 * NB], F32)
        xn1 = sb("xn1", [P, NB, P], F32)
        xn = sb("xn", [P, 2, P], F32)
        x1T = sb("x1T", [P, NB, P], F32)
        x2T = sb("x2T", [P, 2, P], F32)
        x3T = x1T
        x_hi = sb("x_hi", [P, NB, P], F32R)
        x_lo = sb("x_lo", [P, NB, P], F32R)
        ctxT = xn1

        rot = sb("rot", [P, 2, 2, P], F32)
        rot_sw = sb("rot_sw", [P, 2, 2, P], F32)
        qk_f = sb("qk_f", [P, 2, 2, P], F32)
        rest = sb("rest", [P, 2, 2, P], F32)
        parts = sb("parts", [P, 2, 16, P], BF16)
        rest_x = sb("rest_x", [P, 2, 2, P], F32)
        parts_x = sb("parts_x", [P, 2, 16, P], BF16)
        q_room = sb("q_room", [P, NB, NH * P], BF16)
        q_rows = q_room[0:ROWS, :, :].rearrange("p b (h t) -> p b h t", h=NH)
        qx_rows = sb("qx_rows", [ROWS, NB, NH, P], BF16)
        k_rows = sb("k_rows", [ROWS, NB, NH, P], BF16)
        v_aug = sb("v_aug", [P, NB, NH, 32], F32)
        neg_max = sb("neg_max", [P, 2, NH], F32)
        neg_max_h = sb("neg_max_h", [P, 2, 2, NH], BF16)
        shift = sb("shift", [2 * NH, 2, P], BF16)
        nan_fix = sb("nan_fix", [P, 4, NH], F32)
        probs = sb("probs", [P, PR, GH * P], F32)
        r_sb = sb("r_sb", [P, GH * P], F32)
        rden = sb("rden", [P, NH], F32)
        attn_o = sb("attn_o", [P, P], F32)
        attn_oT = sb("attn_oT", [P, P], F32)

        logits = sb("logits", [P, NB, NE], F32)
        top = sb("top", [P, NB, 8], F32)
        top_i = sb("top_i", [P, NB, 8], U32)
        top_f = sb("top_f", [P, NB, 2], F32)
        gap = sb("gap", [P, NB], F32)
        e_gap = sb("e_gap", [P, NB], F32)
        gden = sb("gden", [P, NB], F32)
        prob1 = sb("prob1", [P, NB], F32)
        prob2 = sb("prob2", [P, NB], F32)
        pick1 = sb("pick1", [P, NB, NE], F32)
        pick2 = sb("pick2", [P, NB, NE], F32)
        gates = sb("gates", [P, NB, NE], F32)
        hid = q_room[:, 0:2, :].bitcast(F32).rearrange("p r (c t) -> p r c t", c=NC)
        silu_sb = q_room[:, 2, :].bitcast(F32).rearrange("p (c t) -> p c t", c=NC)
        w13_sb = q_room[:, 3:7, :].bitcast(F32).rearrange("p r x -> p (r x)").rearrange("p (e a h) -> p e a h", a=2, h=NHID)
        w1_sb, w3_sb = w13_sb[:, :, 0, :], w13_sb[:, :, 1, :]

        scratch = nc.dram_tensor("scratch", (NA, 2, P, SLOTS, P), BF16, kind="Internal").ap()

        in_const, in_mask, in_wqkv, in_ctx = sem("in_const"), sem("in_mask"), sem("in_wqkv"), sem("in_ctx")
        in_wx, in_proj, in_gate = sem("in_wx"), sem("in_proj"), sem("in_gate")
        in_w = [sem(f"in_w{i}") for i in range(NE // 2)]
        in_x = [sem("in_x0"), sem("in_x1"), sem("in_x2")]
        const_h = sem("const_h")
        q_zero = [sem(f"q_zero{b}") for b in range(NB)]
        k_zero, k_ones = sem("k_zero"), sem("k_ones")
        qx_zero, qx_ones = sem("qx_zero"), sem("qx_ones")
        v_zero, v_one = [sem("v_zero0"), sem("v_zero1")], sem("v_one")
        w_swapped, turn_ready, turned = sem("w_swapped"), sem("turn_ready"), sem("turned")
        stats_done, rstd_done, veps_done = sem("stats_done"), sem("rstd_done"), sem("veps_done")
        xn1_done, xn_done, bias_added = sem("xn1_done"), sem("xn_done"), sem("bias_added")
        x1T_ready, x1T_taken = sem("x1T_ready"), sem("x1T_taken")
        qkv_ready, rope_done, v_ready, v_taken = sem("qkv_ready"), sem("rope_done"), sem("v_ready"), sem("v_taken")
        sum_done, hi_done, rest_done, mid_done, lo_done, rep_done = (
            sem("sum_done"), sem("hi_done"), sem("rest_done"), sem("mid_done"), sem("lo_done"), sem("rep_done"))
        qkvx_ready, hix_done, vx_taken = sem("qkvx_ready"), sem("hix_done"), sem("vx_taken")
        restx_done, midx_done, lox_done, repx_done = sem("restx_done"), sem("midx_done"), sem("lox_done"), sem("repx_done")
        written = [sem(f"written{n}") for n in range(NA)]
        stacked = [sem(f"stacked{n}") for n in range(NA)]
        shifted = [sem(f"shifted{n}") for n in range(NA)]
        sa_ready, max_done = sem("sa_ready"), sem("max_done")
        nmh_done, nmT_ready, nmT_taken, nan_done = sem("nmh_done"), sem("nmT_ready"), sem("nmT_taken"), sem("nan_done")
        sb_ready, exp_done, masked, pv_done = sem("sb_ready"), sem("exp_done"), sem("masked"), sem("pv_done")
        r_taken, rT_ready, norm_done = sem("r_taken"), sem("rT_ready"), sem("norm_done")
        oT_ready, oT_taken, proj_ready, res_done = sem("oT_ready"), sem("oT_taken"), sem("proj_ready"), sem("res_done")
        xT_ready, xT_taken = sem("xT_ready"), sem("xT_taken")
        gate_ready, logits_taken, gap_done, e_gap_done, gates_done = (
            sem("gate_ready"), sem("logits_taken"), sem("gap_done"), sem("e_gap_done"), sem("gates_done"))
        top_done, pick_done = sem("top_done"), sem("pick_done")
        x_hi_done, x_split, w_hi_done, w_split = sem("x_hi_done"), sem("x_split"), sem("w_hi_done"), sem("w_split")
        up_ready, silu_done, hid_done, down_ready, y_taken = (
            sem("up_ready"), sem("silu_done"), sem("hid_done"), sem("down_ready"), sem("y_taken"))
        y_part, out_done = sem("y_part"), sem("out_done")

        CHUNKS = 2 * NE
        items = []
        for k in range(CHUNKS + 1):
            if k < CHUNKS:
                items += [("up", k, c) for c in range(NC)]
            if k >= 1:
                items.append(("down", k - 1, 0))
        TAIL = NA + 2
        tail_steps = [(n, g) for n in range(NA, TAIL) for g in range(NU)]

        EARLY_UP = (NA - 1, 3)
        FIRST_SPLITS = [(NA - 2, 2), (NA - 1, 3)]
        QX_CLEAR = 8
        GATE_STEP, GATE_ITEM = (NA - 1, 2), 4

        def items_behind(n, g):
            if (n, g) not in tail_steps:
                return []
            at = tail_steps.index((n, g))
            return items[at:at + 1] if at < len(tail_steps) - 1 else items[at:]

        start_banks = [bank_b[0], bank_b[1], bank_r[0], bank_r[1], bank_b[0], bank_b[1]]
        norm_groups = [slice(0, 1), slice(1, HB), slice(HB, NB)]
        NG = len(norm_groups)

        up_banks = [bank_a, bank_b]

        block = stack.enter_context(nc.Block())

        @block.sync
        def _(sp):
            for i, bs in enumerate(norm_groups):
                sp.dma_start(res[:, bs, :], x[bs].rearrange("b t c -> t b c")).then_inc(in_x[i], 16)
                if i == 0:
                    sp.dma_start(consts[:], const).then_inc(in_const, 16)
                    sp.dma_start(wqkv_sb[:], w_qkv).then_inc(in_wqkv, 16)
            sp.dma_start(mask_i[:], mask).then_inc(in_mask, 16)
            for i, w in enumerate((wq, wk, wv, wo)):
                sp.dma_start(wx_sb[:, i, :], w).then_inc(in_wx, 16)
            sp.dma_start(ctx_sb[:], ctx_in.rearrange("b t c -> t b c")).then_inc(in_ctx, 16)
            sp.dma_start(wproj_sb[:], w_proj).then_inc(in_proj, 16)
            sp.dma_start(bias_sb[:], b_proj.rearrange("(o c) -> o c", o=1).to_broadcast([P, P])).then_inc(in_proj, 16)
            sp.dma_start(gate_sb[:], w_gate).then_inc(in_gate, 16)

            def read_rows(n, q_to):
                sp.wait_ge(written[n], 16)
                for t, to in enumerate((q_to, k_rows)):
                    sp.dma_start(to[0:QK_ROWS, n % NB, :, :],
                                 scratch[n, t].rearrange("(h d) s t -> (d s) h t", d=DH)).then_inc(stacked[n], 16)

            sp.wait_ge(const_h, 1)
            sp.wait_ge(k_zero, NB)
            sp.dma_start(k_rows[SHIFT_ROW:SHIFT_ROW + 2, :, :, :],
                         one_rows[:].unsqueeze(1).to_broadcast([2, NB * NH // 4, 4 * P])).then_inc(k_ones, 16)
            sp.dma_start(k_rows[PAD_ROW:PAD_ROW + 1, :, :, :],
                         pad_rows[:].unsqueeze(1).to_broadcast([NB, NH, P])).then_inc(k_ones, 16)
            def write_parts(n):
                tile = parts[:, n % 2] if n < NB else parts_x[:, n % 2]
                sp.wait_ge(lo_done if n < NB else lox_done, n % NB + 1)
                sp.wait_ge(rep_done if n < NB else repx_done, n % NB + 1)
                sp.dma_start(scratch[n].rearrange("a p s t -> p a (s t)"),
                             tile[:, 0:2 * SLOTS, :].rearrange("p (a s) t -> p a (s t)", a=2)).then_inc(written[n], 16)

            def put_shift(n):
                sp.wait_ge(nmT_taken, n + 1)
                sp.wait_ge(sa_ready, NU * (n + 1))
                rows = q_rows if n < NB else qx_rows
                sp.dma_start(rows[SHIFT_ROW:SHIFT_ROW + 2, n % NB, :, :], shift[:, n % 2, :])\
                    .then_inc(shifted[n], 16)


            def stack_self(p):
                sp.wait_ge(q_zero[p], 1)
                read_rows(p, q_rows)

            for p in range(START - 2):
                stack_self(p)
                if p == 2:
                    put_shift(0)
            for n in range(FIRST, NA):
                if 0 <= n + 1 < NA:
                    put_shift(n + 1)
                if n - 2 + LEAD_PREP < NB:
                    stack_self(n - 2 + LEAD_PREP)
                b = n - 4
                if 0 <= b < NB:
                    if b == 0:
                        sp.wait_ge(qx_zero, NB)
                        sp.dma_start(qx_rows[PAD_ROW:PAD_ROW + 1, :, :, :],
                                     one_rows[0:1].unsqueeze(1).to_broadcast([1, NB * NH // 4, 4 * P]))\
                            .then_inc(qx_ones, 16)
                    sp.wait_ge(sb_ready, NU * (b + 1))
                    read_rows(NB + b, qx_rows)
                e = 2 * (n - FIRST_WEIGHTS)
                if e == 0:
                    sp.wait_ge(sb_ready, NB * NU)
                if 0 <= e < NE:
                    sp.dma_start(w1_sb[:, e:e + 2, :], w1[e:e + 2].rearrange("e d h -> d e h")).then_inc(in_w[e // 2], 16)
                    sp.dma_start(w3_sb[:, e:e + 2, :], w3[e:e + 2].rearrange("e d h -> d e h")).then_inc(in_w[e // 2], 16)
                    sp.dma_start(w2_sb[:, e:e + 2], w2[e:e + 2].rearrange("e (c p) d -> p e c d", p=P))\
                        .then_inc(in_w[e // 2], 16)
                if n - 1 + LEAD_PREP < NB:
                    write_parts(n - 1 + LEAD_PREP)
                if 0 <= n - 3 < NB:
                    write_parts(NB + n - 3)
            for bs, sem_, value in ((slice(0, HB), y_taken, NE), (slice(HB, HB + HB // 2), y_part, 1),
                                    (slice(HB + HB // 2, NB), y_taken, 2 * NE)):
                sp.wait_ge(sem_, value)
                sp.dma_start(out[bs].rearrange("b t c -> t b c"), res[:, bs, :]).then_inc(out_done, 16)
            sp.wait_ge(out_done, 48)

        @block.tensor
        def _(pe):
            def transpose_x1(group, bank):
                for i, b in enumerate(range(group.start, group.stop)):
                    pe.wait_ge(xn1_done, b + 1)
                    mm = pe.transpose(bank[:, i * P:(i + 1) * P], xn1[:, b, :], ident)
                mm.then_inc(x1T_ready, 1)

            def project_qk(p, bank):
                for i, w in enumerate((wqkv_sb[:, 0:P], wqkv_sb[:, P:2 * P], wswap[:, 0:P], wswap[:, P:2 * P])):
                    mm = pe.matmul(bank[:, i * P:(i + 1) * P], w, x1T[:, p, :], start=True, stop=True)
                mm.then_inc(qkv_ready, 1)

            def project_v(half, bank):
                for i in range(HB):
                    mm = pe.matmul(bank[:, i * P:(i + 1) * P], x1T[:, half * HB + i, :], wqkv_sb[:, 2 * P:3 * P],
                                   start=True, stop=True)
                mm.then_inc(v_ready, 1)

            def turn(i):
                if i == 0:
                    pe.wait_ge(in_ctx, 16)
                    pe.wait_ge(v_taken, 2)
                else:
                    pe.wait_ge(turned, i)
                if i == 2:
                    pe.wait_ge(in_wx, 64)
                for j in range(4):
                    src = wx_sb[:, j, :] if i == 2 else ctx_sb[:, 4 * i + j, :]
                    mm = pe.transpose(bank_m[:, j * P:(j + 1) * P], src, ident)
                mm.then_inc(turn_ready, 1)

            def scores_a(u):
                n, g = divmod(u, NU)
                b = n % NB
                if g == 0:
                    pe.wait_ge(stacked[n], 32)
                if u == 0:
                    pe.wait_ge(k_ones, 32)
                if u == NB * NU:
                    pe.wait_ge(qx_ones, 16)
                q = q_rows if n < NB else qx_rows
                if u < 2:
                    pe.wait_ge(*((v_taken, 1) if u else (x1T_taken, 2)))
                else:
                    pe.wait_ge(max_done, u - 1)
                bank = bank_a[u % 2]
                for j in range(GH):
                    h = g * GH + j
                    mm = pe.matmul(bank[:, j * P:(j + 1) * P], q[:, b, h, :], k_rows[:, b, h, :],
                                   start=(n < NB or j == 0), stop=(n < NB), skip_group_check=True)
                if n >= NB:
                    mm = pe.matmul(bank[:, :], ident_h[:], causal_h[:].unsqueeze(1).to_broadcast([P, GH, P]),
                                   start=False, stop=True, skip_group_check=True)
                mm.then_inc(sa_ready, 1)

            def scores_b(u):
                n, g = divmod(u, NU)
                b = n % NB
                if g == 0:
                    pe.wait_ge(shifted[n], 16)
                if u >= 2:
                    pe.wait_ge(exp_done, u - 1)
                q = q_rows if n < NB else qx_rows
                for j in range(GH):
                    h = g * GH + j
                    mm = pe.matmul(bank_b[u % 2][:, j * P:(j + 1) * P], k_rows[:, b, h, :], q[:, b, h, :],
                                   start=True, stop=True)
                mm.then_inc(sb_ready, 1)

            def product_v(u):
                n, g = divmod(u, NU)
                if g == 0:
                    if n == 0:
                        pe.wait_ge(v_one, 2)
                    if n < NB:
                        pe.wait_ge(v_taken, n // HB + 1)
                    else:
                        pe.wait_ge(vx_taken, n - NB + 1)
                    if n >= 2:
                        pe.wait_ge(r_taken, n - 1)
                if n < NB:
                    pe.wait_ge(exp_done, u + 1)
                else:
                    pe.wait_ge(masked, u - NB * NU + 1)
                for j in range(GH):
                    mm = pe.matmul(bank_r[n % 2][32 * j:32 * j + 32, g * P:(g + 1) * P],
                                   v_aug[:, n % NB, g * GH + j, :], probs[:, u % PR, j * P:(j + 1) * P],
                                   start=True, stop=True)
                mm.then_inc(pv_done, 1)

            def max_transpose(n):
                pe.wait_ge(nmh_done, n + 1)
                if n == 0:
                    pe.wait_ge(const_h, 1)
                pe.transpose(bank_n[0:2 * NH, 0:P // 2].bitcast(BF16),
                             neg_max_h[:, n % 2, :, :].rearrange("p a h -> p (a h)"), ident_h[:]).then_inc(nmT_ready, 1)

            def up(k, c):
                half, e = divmod(k, NE)
                if k == 0 and c == 0:
                    pe.wait_ge(max_done, UNITS)
                if k == 0 and c == 1:
                    pe.wait_ge(exp_done, UNITS)
                if k >= 1:
                    pe.wait_ge(silu_done, NC * (k - 1) + c + 1)
                    pe.wait_ge(hid_done, NC * (k - 1) + c + 1)
                if e == 0 and c == 0:
                    pe.wait_ge(x_split, HB * (half + 1))
                if c == 0:
                    pe.wait_ge(w_split, k + 1)
                hs, cs = slice(half * HB, (half + 1) * HB), slice(c * P, (c + 1) * P)
                for a, bank in enumerate(up_banks[c]):
                    pe.matmul(bank[:, :], w_lo[:, k % 2, a, cs], x_hi[:, hs, :].rearrange("p b t -> p (b t)"), start=True, stop=False)
                    pe.matmul(bank[:, :], w_hi[:, k % 2, a, cs], x_lo[:, hs, :].rearrange("p b t -> p (b t)"), start=False, stop=False)
                    mm = pe.matmul(bank[:, :], w_hi[:, k % 2, a, cs], x_hi[:, hs, :].rearrange("p b t -> p (b t)"),
                                   start=False, stop=True)
                mm.then_inc(up_ready, 1)

            def down(k):
                if k == 0:
                    pe.wait_ge(r_taken, NA)
                if k >= 2:
                    pe.wait_ge(y_taken, k - 1)
                pe.wait_ge(hid_done, NC * (k + 1))
                for bb in range(HB):
                    for c in range(NC):
                        mm = pe.matmul(bank_r[k % 2][:, bb * P:(bb + 1) * P], hid[:, k % 2, c, bb * P:(bb + 1) * P],
                                       w2_sb[:, k % NE, c, :], start=(c == 0), stop=(c == NC - 1))
                mm.then_inc(down_ready, 1)

            pe.wait_ge(in_const, 16)
            transpose_x1(norm_groups[0], bank_n)
            pe.wait_ge(in_wqkv, 16)
            pe.wait_ge(w_swapped, 1)
            pe.wait_ge(x1T_taken, 1)
            project_qk(0, start_banks[0])
            transpose_x1(norm_groups[1], bank_a[0])
            pe.wait_ge(x1T_taken, 2)
            for p in range(1, HB):
                project_qk(p, start_banks[p])
            transpose_x1(norm_groups[2], bank_m)
            project_v(0, bank_a[1])
            pe.wait_ge(x1T_taken, 3)
            for p in range(HB, START):
                pe.wait_ge(rope_done, p - HB + 1)
                project_qk(p, start_banks[p])
            project_v(1, bank_m)
            for u in range(LEAD_UNITS):
                scores_a(u)
                if u in (1, 3, 5):
                    turn(u // 2)
                if u == NU - 1:
                    max_transpose(0)
            for n in range(FIRST, TAIL):
                for g in range(NU):
                    u = n * NU + g
                    if 0 <= u + LEAD_UNITS < UNITS:
                        scores_a(u + LEAD_UNITS)
                    if 0 <= u < UNITS:
                        scores_b(u)
                    if 0 <= u - LAG < UNITS:
                        product_v(u - LAG)
                    if g == 0 and 2 <= n <= NA + 1:
                        pe.wait_ge(oT_taken, n - 1)
                        if n == 2:
                            pe.wait_ge(in_proj, 32)
                        pe.matmul(bank_m[:, 0:P], attn_oT[:], wproj_sb[:] if n - 2 < NB else wxT[:, 3, :],
                                  start=True, stop=True).then_inc(proj_ready, 1)
                    if g == 0:
                        if 0 <= n + 1 < NA:
                            if n == FIRST:
                                pe.wait_ge(nmT_taken, n + 1)
                            if n - 1 + LEAD_PREP < NB:
                                pe.wait_ge(rope_done, n + LEAD_PREP)
                            if 0 <= n - 3 < NB:
                                pe.wait_ge(vx_taken, n - 2)
                                pe.wait_ge(restx_done, n - 2)
                            if n - 1 >= NB + 2:
                                pe.wait_ge(logits_taken, n - NB - 2)
                            max_transpose(n + 1)
                    if g == 2:
                        if n + LEAD_PREP < NB:
                            pe.wait_ge(nmT_taken, n + 2)
                            project_qk(n + LEAD_PREP, bank_n)
                        if 1 <= n <= NA:
                            if n == 1:
                                pe.wait_ge(turned, 3)
                            if n >= 2:
                                pe.wait_ge(res_done, n - 1)
                            pe.wait_ge(r_taken, n)
                            for i in range(GH):
                                mm = pe.transpose(bank_m[:, i * P:(i + 1) * P], r_sb[:, i * P:(i + 1) * P], ident)
                            mm.then_inc(rT_ready, 1)
                        if n >= 2:
                            if n + 1 < NA:
                                pe.wait_ge(nmT_taken, n + 2)
                            else:
                                pe.wait_ge(logits_taken, n - NB - 2)
                            pe.wait_ge(xn_done, n - 1)
                            pe.transpose(bank_n[:, P:2 * P], xn[:, n % 2, :], ident).then_inc(xT_ready, 1)
                    if g == 3:
                        if n + LEAD_PREP < NB:
                            if n >= 2:
                                pe.wait_ge(rope_done, n + LEAD_PREP + 1)
                        elif n + 1 < NA:
                            pe.wait_ge(nmT_taken, n + 2)
                        if 0 <= n - 2 < NB:
                            m = n - 2
                            pe.wait_ge(xT_taken, m + 1)
                            pe.matmul(bank_n[:, 0:P], wxT[:, 0, :], x2T[:, m % 2, :], start=True, stop=True)
                            pe.matmul(bank_n[:, P:2 * P], wxT[:, 1, :], ctxT[:, m, :], start=True, stop=True)
                            pe.matmul(bank_n[:, 2 * P:3 * P], ctxT[:, m, :], wxT[:, 2, :], start=True, stop=True)\
                                .then_inc(qkvx_ready, 1)
                        if n - 2 >= NB:
                            m = n - 2 - NB
                            if n == NB + 2:
                                pe.wait_ge(in_gate, 16)
                            if m >= 1:
                                pe.wait_ge(logits_taken, m)
                            pe.wait_ge(xT_taken, n - 1)
                            pe.matmul(bank_n[:, 0:NE], x3T[:, m, :], gate_sb[:], start=True, stop=True)\
                                .then_inc(gate_ready, 1)
                        if 1 <= n <= NA:
                            pe.wait_ge(norm_done, n)
                            pe.transpose(bank_m[:, 0:P], attn_o[:], ident).then_inc(oT_ready, 1)
                    if (n, g) == EARLY_UP:
                        up(0, 0)
                    for kind, k, c in items_behind(n, g):
                        if (kind, k, c) == ("up", 0, 0):
                            continue
                        if kind == "up":
                            up(k, c)
                        else:
                            down(k)

        @block.scalar
        def _(act):
            def clear(rows, b, done):
                act.memzero(rows[:, b].rearrange("p h t -> p (h t)")).then_inc(done, 1)

            def copy_x1T(i, bank):
                act.wait_ge(x1T_ready, i + 1)
                count = norm_groups[i].stop - norm_groups[i].start
                act.activation(x1T[:, norm_groups[i], :], bank[:, 0:count * P].rearrange("p (b t) -> p b t", t=P), ACT.Copy)\
                    .then_inc(x1T_taken, 1)

            def copy_v(half, bank):
                act.wait_ge(v_ready, half + 1)
                act.wait_ge(v_zero[half], 1)
                act.activation(v_aug[:, half * HB:(half + 1) * HB, :, 0:DH],
                               bank[:, :].rearrange("p (b h d) -> p b h d", b=HB, d=DH), ACT.Copy).then_inc(v_taken, 1)

            def hi_self(p):
                act.wait_ge(sum_done, p + 1)
                if p >= 2:
                    act.wait_ge(written[p - 2], 16)
                act.activation(parts[:, p % 2, 0:9:8, :], qk_f[:, p % 2], ACT.Copy).then_inc(hi_done, 1)

            def mid_self(p):
                act.wait_ge(rest_done, p + 1)
                act.activation(parts[:, p % 2, 3:8:4, :], rest[:, p % 2], ACT.Copy).then_inc(mid_done, 1)

            def hi_cross(m):
                act.wait_ge(qkvx_ready, m + 1)
                act.wait_ge(pv_done, NU * (m + 1))
                act.activation(v_aug[:, m, :, 0:DH], bank_n[:, 2 * P:3 * P].rearrange("p (h d) -> p h d", h=NH), ACT.Copy)\
                    .then_inc(vx_taken, 1)
                if m >= 2:
                    act.wait_ge(written[NB + m - 2], 16)
                act.activation(parts_x[:, m % 2, 0:9:8, :], bank_n[:, 0:2 * P].rearrange("p (a t) -> p a t", a=2), ACT.Copy)\
                    .then_inc(hix_done, 1)

            def mid_cross(m):
                act.wait_ge(restx_done, m + 1)
                act.activation(parts_x[:, m % 2, 3:8:4, :], rest_x[:, m % 2], ACT.Copy).then_inc(midx_done, 1)

            def write_start(n):
                tile = parts[:, n % 2]
                act.wait_ge(lo_done, n + 1)
                act.wait_ge(rep_done, n + 1)
                act.dma_start(scratch[n].rearrange("a p s t -> p a (s t)"),
                             tile[:, 0:2 * SLOTS, :].rearrange("p (a s) t -> p a (s t)", a=2)).then_inc(written[n], 16)

            def take_max(n):
                act.wait_ge(nmT_ready, n + 1)
                if n >= 2:
                    act.wait_ge(shifted[n - 2], 16)
                act.activation(shift[:, n % 2, :], bank_n[0:2 * NH, 0:P // 2].bitcast(BF16), ACT.Copy).then_inc(nmT_taken, 1)

            def exp_gap(half):
                hs = slice(half * HB, (half + 1) * HB)
                act.wait_ge(gap_done, half + 1)
                act.activation(e_gap[:, hs], gap[:, hs], ACT.Exp).then_inc(e_gap_done, 1)

            def silu(k, c):
                act.wait_ge(up_ready, NC * k + c + 1)
                if k >= 1:
                    act.wait_ge(hid_done, NC * (k - 1) + c + 1)
                elif c == 0:
                    act.wait_ge(sb_ready, NB * NU)
                act.activation(silu_sb[:, c, :], up_banks[c][0][:, :], ACT.Silu).then_inc(silu_done, 1)

            for b in range(2, 5):
                clear(k_rows, b, k_zero)
            def turn(i):
                act.wait_ge(turn_ready, i + 1)
                act.activation(wxT[:] if i == 2 else ctxT[:, 4 * i:4 * (i + 1), :],
                               bank_m[:, :].rearrange("p (a t) -> p a t", a=4), ACT.Copy).then_inc(turned, 1)

            copy_x1T(0, bank_n)
            act.memzero(v_aug[:, 0:HB].rearrange("p b h c -> p (b h c)")).then_inc(v_zero[0], 1)
            copy_x1T(1, bank_a[0])
            hi_self(0)
            mid_self(0)
            write_start(0)
            clear(q_rows, 1, q_zero[1])
            hi_self(1)
            mid_self(1)
            copy_x1T(2, bank_m)
            write_start(1)
            copy_v(0, bank_a[1])
            hi_self(2)
            mid_self(2)
            clear(q_rows, 2, q_zero[2])
            copy_v(1, bank_m)
            hi_self(3)
            turn(0)
            write_start(2)
            mid_self(3)
            turn(1)
            write_start(3)
            take_max(0)
            hi_self(4)
            mid_self(4)
            turn(2)
            hi_self(5)
            write_start(4)

            for n in range(FIRST, TAIL):
                for g in range(NU):
                    u = n * NU + g
                    if g == 1:
                        if 1 <= n <= NA:
                            act.wait_ge(pv_done, NU * n)
                            if n >= 2:
                                act.wait_ge(rT_ready, n - 1)
                            act.activation(r_sb[:], bank_r[(n - 1) % 2][:, :], ACT.Copy).then_inc(r_taken, 1)
                    if 0 <= u < UNITS:
                        act.wait_ge(sb_ready, u + 1)
                        if u >= PR:
                            act.wait_ge(pv_done, u - PR + 1)
                        act.activation(probs[:, u % PR, :], bank_b[u % 2][:, :], ACT.Exp, scale=SCALE)\
                            .then_inc(exp_done, 1)
                    if g == 0 and 0 <= n + 1 < NA:
                        take_max(n + 1)
                    if g == 1:
                        if 0 <= n - 1 + LEAD_PREP < NB:
                            mid_self(n - 1 + LEAD_PREP)
                        if 0 <= n - 3 < NB:
                            mid_cross(n - 3)
                    if g == 2:
                        if n >= 2:
                            m = n - 2
                            act.wait_ge(xT_ready, m + 1)
                            if 2 <= m < NB:
                                act.wait_ge(qkvx_ready, m - 1)
                            if m >= NB:
                                act.activation(x_hi[:, m - NB, :], bank_n[:, P:2 * P], ACT.Copy).then_inc(x_hi_done, 1)
                            act.activation(x2T[:, m % 2, :] if m < NB else x3T[:, m - NB, :], bank_n[:, P:2 * P],
                                           ACT.Copy).then_inc(xT_taken, 1)
                    if g == 3:
                        if n + LEAD_PREP < NB:
                            hi_self(n + LEAD_PREP)
                        if 0 <= n - 2 < NB:
                            hi_cross(n - 2)
                        if 1 <= n <= NA:
                            act.wait_ge(oT_ready, n)
                            if n >= 2:
                                act.wait_ge(proj_ready, n - 1)
                            act.activation(attn_oT[:], bank_m[:, 0:P], ACT.Copy).then_inc(oT_taken, 1)
                    if (n, g) == GATE_STEP:
                        exp_gap(0)
                    for kind, k, c in items_behind(n, g):
                        if (kind, k) == ("down", GATE_ITEM):
                            exp_gap(1)
                        if kind == "up":
                            silu(k, c)

        @block.vector
        def _(dve):
            steps = [0]
            dve_step = sem("dve_step")

            def then(ins):
                steps[0] += 1
                ins.then_inc(dve_step, 1)
                dve.wait_ge(dve_step, steps[0])

            def repeat(tile):
                by8 = tile.rearrange("p (a s) t -> p a s t", a=2)
                dve.tensor_copy(by8[:, :, 1:3, :], by8[:, :, 0:1, :].to_broadcast([P, 2, 2, P]))
                return dve.tensor_copy(tile[:, 5:12:6, :], tile[:, 3:8:4, :])

            def repeat_self(p):
                dve.wait_ge(mid_done, p + 1)
                repeat(parts[:, p % 2]).then_inc(rep_done, 1)

            def norm_stats(src, slot):
                then(dve.bn_stats(stats[:, slot, :], src))
                dve.bn_aggr(mv[:, slot, :], stats[:, slot, :]).then_inc(stats_done, 1)

            def normalise(dst, src, slot, done):
                dve.tensor_scalar(dst, src, mv[:, slot, 0:1], rstd[:, slot:slot + 1], ALU.subtract, ALU.mult)\
                    .then_inc(done, 1)

            def maximum(u):
                n, g = divmod(u, NU)
                dve.wait_ge(sa_ready, u + 1)
                if g == 0 and n >= 2:
                    dve.wait_ge(nmh_done, n - 1)
                    if n >= NB + 2:
                        dve.wait_ge(nan_done, n - 1 - NB)
                dve.tensor_reduce(neg_max[:, n % 2, g * GH:(g + 1) * GH],
                                  bank_a[u % 2][:, :].rearrange("p (h k) -> p h k", h=GH), AX.X, ALU.max, negate=True)\
                    .then_inc(max_done, 1)

            def split_max(n):
                dve.wait_ge(max_done, NU * (n + 1))
                if n >= 2:
                    dve.wait_ge(nmT_ready, n - 1)
                then(dve.tensor_copy(neg_max_h[:, n % 2, 0, :], neg_max[:, n % 2, :]))
                dve.tensor_tensor(neg_max_h[:, n % 2, 1, :], neg_max[:, n % 2, :], neg_max_h[:, n % 2, 0, :],
                                  ALU.subtract).then_inc(nmh_done, 1)
                if n >= NB:
                    if n >= NB + 4:
                        dve.wait_ge(norm_done, n - 3)
                    dve.tensor_scalar(nan_fix[:, n % 4, :], neg_max[:, n % 2, :], 1e10, 0.0, ALU.mult, ALU.mult)\
                        .then_inc(nan_done, 1)

            def rope(p, bank):
                dve.wait_ge(qkv_ready, p + 1)
                if p >= 2:
                    dve.wait_ge(sum_done, p - 1)
                v = bank[:, :].rearrange("p (a t) -> p a t", a=4)
                dve.tensor_tensor(rot[:, p % 2], v[:, 0:2, :], cos_t.unsqueeze(1).to_broadcast([P, 2, P]), ALU.mult)
                dve.tensor_tensor(rot_sw[:, p % 2], v[:, 2:4, :], sin_t.unsqueeze(1).to_broadcast([P, 2, P]), ALU.mult)\
                    .then_inc(rope_done, 1)

            def rest_self(p):
                dve.wait_ge(sum_done, p + 1)
                dve.wait_ge(hi_done, p + 1)
                if p >= 2:
                    dve.wait_ge(lo_done, p - 1)
                dve.tensor_tensor(rest[:, p % 2], qk_f[:, p % 2], parts[:, p % 2, 0:9:8, :],
                                   ALU.subtract).then_inc(rest_done, 1)

            def lo_self(p):
                dve.wait_ge(rest_done, p + 1)
                dve.wait_ge(mid_done, p + 1)
                dve.tensor_tensor(parts[:, p % 2, 4:7:2, :], rest[:, p % 2], parts[:, p % 2, 3:8:4, :], ALU.subtract).then_inc(lo_done, 1)

            def divide(n):
                dve.wait_ge(rT_ready, n + 1)
                v = bank_m[:, :].rearrange("p (h c) -> p h c", c=32)
                then(dve.reciprocal(rden[:], v[:, :, DH]))
                if n >= NB:
                    dve.wait_ge(nan_done, n - NB + 1)
                    then(dve.tensor_tensor(rden[:], rden[:], nan_fix[:, n % 4, :], ALU.add))
                if n >= 1:
                    dve.wait_ge(oT_ready, n)
                dve.tensor_tensor(attn_o[:].rearrange("p (h d) -> p h d", h=NH), v[:, :, 0:DH],
                                  rden[:].unsqueeze(2).to_broadcast([P, NH, DH]), ALU.mult).then_inc(norm_done, 1)

            def add_residual(n):
                b = n % NB
                dve.wait_ge(proj_ready, n + 1)
                if n % HB == 0 and n < NB:
                    dve.wait_ge(bias_added, n // HB + 1)
                if n >= NB:
                    dve.wait_ge(res_done, n - NB + 1)
                dve.tensor_tensor(res[:, b, :], bank_m[:, 0:P], res[:, b, :], ALU.add).then_inc(res_done, 1)
                dve.wait_ge(res_done, n + 1)
                norm_stats(res[:, b, :], NB + n)

            def two_largest(b):
                dve.wait_ge(logits_taken, b + 1)
                then(dve.max(out=top[:, b, :], in_=logits[:, b, :]))
                dve.max_index(out=top_i[:, b, :], in_max=top[:, b, :], in_values=logits[:, b, :]).then_inc(top_done, 1)

            def picks(half):
                hs = slice(half * HB, (half + 1) * HB)
                wide = [P, HB, NE]
                dve.wait_ge(top_done, HB * (half + 1))
                dve.tensor_tensor(gap[:, hs], top[:, hs, 1], top[:, hs, 0], ALU.subtract).then_inc(gap_done, 1)
                then(dve.tensor_copy(top_f[:, hs, :], top_i[:, hs, 0:2]))
                for i, pick in enumerate((pick1, pick2)):
                    dve.tensor_tensor(pick[:, hs, :], iota.unsqueeze(1).to_broadcast(wide),
                                      top_f[:, hs, i].unsqueeze(2).to_broadcast(wide), ALU.is_equal).then_inc(pick_done, 1)

            def gate_values(half):
                hs = slice(half * HB, (half + 1) * HB)
                wide = [P, HB, NE]
                dve.wait_ge(e_gap_done, half + 1)
                dve.wait_ge(pick_done, 2 * (half + 1))
                then(dve.tensor_scalar(gden[:, hs], e_gap[:, hs], 1.0, None, ALU.add))
                then(dve.reciprocal(prob1[:, hs], gden[:, hs]))
                dve.tensor_tensor(pick1[:, hs, :], pick1[:, hs, :], prob1[:, hs].unsqueeze(2).to_broadcast(wide), ALU.mult)
                then(dve.tensor_tensor(prob2[:, hs], e_gap[:, hs], prob1[:, hs], ALU.mult))
                then(dve.tensor_tensor(pick2[:, hs, :], pick2[:, hs, :], prob2[:, hs].unsqueeze(2).to_broadcast(wide), ALU.mult))
                dve.tensor_tensor(gates[:, hs, :], pick1[:, hs, :], pick2[:, hs, :], ALU.add).then_inc(gates_done, 1)

            def split_first_w(k):
                if k == 0:
                    dve.wait_ge(in_w[0], 48)
                dve.tensor_scalar(w_hi[:, k], w13_sb[:, k], 1.0, 1.0, ALU.mult, ALU.mult).then_inc(w_hi_done, 1)
                dve.wait_ge(w_hi_done, k + 1)
                dve.tensor_tensor(w_lo[:, k], w13_sb[:, k], w_hi[:, k].bitcast(F32), ALU.subtract).then_inc(w_split, 1)

            def hidden(k, c):
                dve.wait_ge(silu_done, NC * k + c + 1)
                if k == 0 and c == 0:
                    dve.wait_ge(sb_ready, NB * NU)
                if k >= 2 and c == 0:
                    dve.wait_ge(down_ready, k - 1)
                dve.tensor_tensor(hid[:, k % 2, c, :], up_banks[c][1][:, :], silu_sb[:, c, :], ALU.mult).then_inc(hid_done, 1)

            def add_expert(k):
                half, e = divmod(k, NE)
                dve.wait_ge(down_ready, k + 1)
                if e == 0:
                    dve.wait_ge(gates_done, half + 1)
                    dve.wait_ge(res_done, NB + HB * (half + 1))
                if k >= 1:
                    dve.wait_ge(y_taken, k)
                for bb in range(HB):
                    b = half * HB + bb
                    ins = dve.scalar_tensor_tensor(out=res[:, b, :], in0=bank_r[k % 2][:, bb * P:(bb + 1) * P],
                                                   scalar=gates[:, b, e:e + 1], in1=res[:, b, :],
                                                   op0=ALU.mult, op1=ALU.add)
                    if k == CHUNKS - 1 and bb == HB // 2 - 1:
                        ins.then_inc(y_part, 1)
                ins.then_inc(y_taken, 1)

            dve.memset(one_rows[:].bitcast(U32), ONES)
            for b in range(2):
                dve.memset(k_rows[:, b].bitcast(U32), 0).then_inc(k_zero, 1)
            dve.memset(q_rows[:, 0].bitcast(U32), 0).then_inc(q_zero[0], 1)
            dve.wait_ge(in_x[0], 16)
            norm_stats(res[:, 0, :], 0)
            dve.wait_ge(in_const, 16)
            dve.wait_ge(in_wqkv, 16)
            src = wqkv_sb[:, 0:2 * P].rearrange("p (h s j) -> p h s j", s=2, j=DH // 2)
            dst = wswap[:].rearrange("p (h s j) -> p h s j", s=2, j=DH // 2)
            dve.tensor_copy(dst[:, :, 0, :], src[:, :, 1, :])
            dve.tensor_copy(dst[:, :, 1, :], src[:, :, 0, :]).then_inc(w_swapped, 1)
            dve.wait_ge(rstd_done, 1)
            normalise(xn1[:, 0, :], res[:, 0, :], 0, xn1_done)
            dve.wait_ge(in_x[1], 16)
            for b in range(1, HB):
                norm_stats(res[:, b, :], b)
            dve.tensor_copy(ident_h[:], ident)
            dve.tensor_copy(causal_h[:], causal_f)
            dve.wait_ge(in_mask, 16)
            dve.tensor_scalar(pad_rows[:], mask_i[:], 0.0, -BIG, ALU.is_equal, ALU.mult).then_inc(const_h, 1)
            dve.wait_ge(rstd_done, 2)
            for b in range(1, HB):
                normalise(xn1[:, b, :], res[:, b, :], b, xn1_done)
            dve.wait_ge(v_zero[0], 1)
            dve.memset(v_aug[:, 0:HB, :, DH], 1.0).then_inc(v_one, 1)
            rope(0, start_banks[0])
            dve.wait_ge(in_x[2], 16)
            for b in range(HB, NB):
                norm_stats(res[:, b, :], b)
            rest_self(0)
            lo_self(0)
            repeat_self(0)
            rope(1, start_banks[1])
            dve.wait_ge(rstd_done, NG)
            for b in range(HB, NB):
                normalise(xn1[:, b, :], res[:, b, :], b, xn1_done)
            rest_self(1)
            rope(2, start_banks[2])
            lo_self(1)
            repeat_self(1)
            rope(3, start_banks[3])
            rope(4, start_banks[4])
            rest_self(2)
            repeat_self(2)
            dve.wait_ge(v_zero[1], 1)
            dve.memset(v_aug[:, HB:NB, :, DH], 1.0).then_inc(v_one, 1)
            maximum(0)
            maximum(1)
            rope(5, start_banks[5])
            rest_self(3)
            maximum(2)
            repeat_self(3)
            maximum(3)
            split_max(0)
            maximum(4)
            maximum(5)
            repeat_self(4)
            maximum(6)
            maximum(7)
            split_max(1)
            maximum(8)

            for n in range(FIRST, TAIL):
                for g in range(NU):
                    u = n * NU + g
                    if 0 <= u + LEAD_UNITS < UNITS:
                        maximum(u + LEAD_UNITS)
                    if g == 3 and 0 <= n + 2 < NA:
                        split_max(n + 2)
                    if g == 0 and 2 <= n <= NA + 1:
                        add_residual(n - 2)
                    if g == 1:
                        if n >= 2:
                            dve.wait_ge(rstd_done, NG + n - 1)
                            if n >= 4:
                                dve.wait_ge(xT_ready, n - 3)
                            normalise(xn[:, n % 2, :], res[:, (n - 2) % NB, :], NB + n - 2, xn_done)
                    if g == 2:
                        if 1 <= n <= NA:
                            divide(n - 1)
                        if 0 <= n - 1 + LEAD_PREP < NB:
                            repeat_self(n - 1 + LEAD_PREP)
                        if n + LEAD_PREP < NB:
                            rope(n + LEAD_PREP, bank_n)
                        if 0 <= n - 3 < NB:
                            dve.wait_ge(midx_done, n - 2)
                            repeat(parts_x[:, (n - 3) % 2]).then_inc(repx_done, 1)
                    if g == 3:
                        if 0 <= n - 2 < NB:
                            m = n - 2
                            dve.wait_ge(hix_done, m + 1)
                            if m >= 2:
                                dve.wait_ge(lox_done, m - 1)
                            dve.tensor_tensor(rest_x[:, m % 2], bank_n[:, 0:2 * P].rearrange("p (a t) -> p a t", a=2),
                                              parts_x[:, m % 2, 0:9:8, :], ALU.subtract).then_inc(restx_done, 1)
                        if n - 2 >= NB:
                            m = n - 2 - NB
                            dve.wait_ge(gate_ready, m + 1)
                            dve.tensor_copy(logits[:, m, :], bank_n[:, 0:NE]).then_inc(logits_taken, 1)
                            two_largest(m)
                            if m % HB == HB - 1:
                                picks(m // HB)
                    if (n, g) == GATE_STEP:
                        gate_values(0)
                    if (n, g) in FIRST_SPLITS:
                        split_first_w(FIRST_SPLITS.index((n, g)))
                    for kind, k, c in items_behind(n, g):
                        if (kind, k) == ("down", GATE_ITEM):
                            gate_values(1)
                        if kind == "up":
                            hidden(k, c)
                        else:
                            add_expert(k)

        @block.gpsimd
        def _(pool):
            def clear(rows, b, done):
                pool.memset(rows[:, b].bitcast(U32), 0).then_inc(done, 1)

            def inverse_std(slots, count):
                pool.wait_ge(stats_done, slots.stop)
                pool.tensor_scalar(veps[:, slots], mv[:, slots, 1], EPS, 1.0, ALU.add, ALU.mult).then_inc(veps_done, 1)
                pool.wait_ge(veps_done, count)
                pool.tensor_tensor(rstd[:, slots], veps[:, slots], minus_half[:, 0:slots.stop - slots.start], ALU.pow)\
                    .then_inc(rstd_done, 1)

            def sum_self(p):
                pool.wait_ge(rope_done, p + 1)
                if p >= 2:
                    pool.wait_ge(hi_done, p - 1)
                    pool.wait_ge(rest_done, p - 1)
                pool.tensor_tensor(qk_f[:, p % 2], rot[:, p % 2], rot_sw[:, p % 2], ALU.add).then_inc(sum_done, 1)

            def rest_self(p):
                pool.wait_ge(sum_done, p + 1)
                pool.wait_ge(hi_done, p + 1)
                if p >= 2:
                    pool.wait_ge(lo_done, p - 1)
                pool.tensor_tensor(rest[:, p % 2], qk_f[:, p % 2], parts[:, p % 2, 0:9:8, :],
                                   ALU.subtract).then_inc(rest_done, 1)

            def lo_self(p):
                pool.wait_ge(rest_done, p + 1)
                pool.wait_ge(mid_done, p + 1)
                pool.tensor_tensor(parts[:, p % 2, 4:7:2, :], rest[:, p % 2], parts[:, p % 2, 3:8:4, :], ALU.subtract).then_inc(lo_done, 1)

            def split_x(m):
                pool.wait_ge(x_hi_done, m + 1)
                pool.wait_ge(xT_taken, NB + m + 1)
                pool.tensor_tensor(x_lo[:, m, :], x3T[:, m, :], x_hi[:, m, :].bitcast(F32), ALU.subtract).then_inc(x_split, 1)

            def split_w(k):
                e = k % NE
                if k < NE and e % 2 == 0:
                    pool.wait_ge(in_w[e // 2], 48)
                pool.wait_ge(up_ready, NC * (k - 1))
                pool.tensor_scalar(w_hi[:, k % 2], w13_sb[:, e], 1.0, 1.0, ALU.mult, ALU.mult).then_inc(w_hi_done, 1)
                pool.wait_ge(w_hi_done, k + 1)
                pool.tensor_tensor(w_lo[:, k % 2], w13_sb[:, e], w_hi[:, k % 2].bitcast(F32), ALU.subtract).then_inc(w_split, 1)

            for b in range(5, NB):
                clear(k_rows, b, k_zero)
            clear(q_rows, 3, q_zero[3])
            pool.wait_ge(in_const, 16)
            inverse_std(norm_groups[0], 1)
            inverse_std(norm_groups[1], 2)
            pool.memset(v_aug[:, HB:NB], 0.0).then_inc(v_zero[1], 1)
            sum_self(0)
            inverse_std(norm_groups[2], 3)
            sum_self(1)
            sum_self(2)
            sum_self(3)
            lo_self(2)
            sum_self(4)
            lo_self(3)
            rest_self(4)
            clear(q_rows, 4, q_zero[4])
            sum_self(5)
            lo_self(4)
            rest_self(5)
            clear(q_rows, 5, q_zero[5])

            for n in range(FIRST, TAIL):
                for g in range(NU):
                    u = n * NU + g
                    if NB * NU <= u < UNITS:
                        pool.wait_ge(exp_done, u + 1)
                        pool.affine_select(out=probs[:, u % PR, :], in_=probs[:, u % PR, :], compare_op=ALU.is_ge,
                                           fill=0.0, base=0, pattern=[[0, GH], [1, P]], channel_multiplier=-1)\
                            .then_inc(masked, 1)
                    if g == 0 and n >= 2:
                        inverse_std(slice(NB + n - 2, NB + n - 1), NG + n - 1)
                    if g == 1:
                        if 0 <= n - 1 + LEAD_PREP < NB:
                            lo_self(n - 1 + LEAD_PREP)
                        if 0 <= n - 3 < NB:
                            m = n - 3
                            pool.wait_ge(midx_done, m + 1)
                            pool.tensor_tensor(parts_x[:, m % 2, 4:7:2, :], rest_x[:, m % 2], parts_x[:, m % 2, 3:8:4, :],
                                               ALU.subtract).then_inc(lox_done, 1)
                    if g == 3 and n + LEAD_PREP < NB:
                        sum_self(n + LEAD_PREP)
                        rest_self(n + LEAD_PREP)
                    if g == 1 and n + LEAD_PREP < NB:
                        clear(q_rows, n + LEAD_PREP, q_zero[n + LEAD_PREP])
                    if 0 <= u - QX_CLEAR < NB:
                        clear(qx_rows, u - QX_CLEAR, qx_zero)
                    if g == 2 and n >= NB + 2:
                        split_x(n - 2 - NB)
                    for kind, k, c in items_behind(n, g):
                        if kind == "up" and c == NC - 1 and k + 2 < CHUNKS:
                            split_w(k + 2)
                    if g == 3 and n in (0, 2):
                        if n == 0:
                            pool.wait_ge(in_proj, 32)
                            pool.wait_ge(xn1_done, NB)
                        hs = slice(n // 2 * HB, (n // 2 + 1) * HB)
                        pool.tensor_tensor(res[:, hs, :], res[:, hs, :], bias_sb[:].unsqueeze(1).to_broadcast([P, HB, P]),
                                           ALU.add).then_inc(bias_added, 1)


_INS = ['x', 'ctx_1024', 'mask_BxS2_if1', 'L0_attn_w_qkv', 'L0_attn_w_proj', 'L0_attn_b_proj',
        'L0_xattn_Wq', 'L0_xattn_Wk', 'L0_xattn_Wv', 'L0_xattn_Wo',
        'L0_ffn_w_gate', 'L0_ffn_w1', 'L0_ffn_w3', 'L0_ffn_w2']


def _constants():
    import numpy as np
    c = np.zeros((P, NCONST), np.float32)
    c[:, C_ID:C_ID + P] = np.eye(P, dtype=np.float32)
    c[:, C_CAUSAL:C_CAUSAL + P] = np.where(np.tril(np.ones((P, P), bool)), 0.0, -BIG)
    inv = (1.0 / np.float32(10000.0) ** (np.arange(0, DH, 2, dtype=np.float32) / np.float32(DH))).astype(np.float32)
    ang = (np.arange(P, dtype=np.float32)[:, None] * inv[None, :]).astype(np.float32)
    f = np.arange(P)
    sign = np.where(f % DH < DH // 2, -1.0, 1.0).astype(np.float32)
    c[:, C_COS:C_COS + P] = np.cos(ang).T[f % (DH // 2)]
    c[:, C_SIN:C_SIN + P] = np.sin(ang).T[f % (DH // 2)] * sign[:, None]
    c[:, C_IOTA:C_IOTA + NE] = np.arange(NE)
    c[:, C_HALF:C_HALF + NE] = -0.5
    return c


def kernel(**inputs):
    import numpy as _np
    import concourse.bacc as _bacc
    from concourse import mybir as _mybir
    from concourse.bass_utils import run_bass_kernel_spmd as _run

    nc = _bacc.Bacc("TRN2", target_bir_lowering=False, num_devices=1)
    arrays, args = {}, []
    named = [(name, _np.ascontiguousarray(inputs[name])) for name in _INS] + [("const", _constants())]
    for name, a in named:
        arrays[f"in_{name}_dram"] = a
        args.append(nc.dram_tensor(f"in_{name}_dram", a.shape, _mybir.dt.from_np(a.dtype), kind="ExternalInput").ap())
    args.append(nc.dram_tensor("out_0_dram", (NB, P, P), _mybir.dt.float32, kind="ExternalOutput").ap())
    decoder_block(nc, *args)
    r = _run(nc, [arrays], core_ids=[0])
    return r.results[0]["out_0_dram"]
```
